# Optimizing a Trainium2 kernel written in Bass

```python
import numpy as np
import jax
import jax.numpy as jnp

def _softmax(x, axis=-1):
    return jax.nn.softmax(x, axis=axis)

def _gelu(x):
    return jax.nn.gelu(x, approximate=True)

def _silu(x):
    return jax.nn.silu(x)

def _sigmoid(x):
    return jax.nn.sigmoid(x)

def _layernorm(x, axis=-1, eps=1e-05):
    m = jnp.mean(x, axis=axis, keepdims=True)
    v = jnp.var(x, axis=axis, keepdims=True)
    return (x - m) / jnp.sqrt(v + eps)

def _scatter_add(tgt, idx, src, axis=0):
    return tgt.at[idx].add(src)

def _segment_sum(src, seg, n):
    return jax.ops.segment_sum(src, seg, n)
kernel_name = 'mk_gnn_resnorm_d1_gnn_r8_d672a9'

def setup_inputs(seed: int=0):
    np.random.seed(seed)
    _w = jnp.asarray

    def _rec_inputs():
        import jax
        import jax.numpy as jnp
        _gk = jax.random.key(seed)
        x = -8.776e-05 + 1 * jax.random.normal(jax.random.fold_in(_gk, 1), (2500, 256), jnp.float32)
        src = jax.random.randint(jax.random.fold_in(_gk, 2), (80000,), 0, 2500, jnp.int32)
        dst = jnp.minimum((2500 * jax.random.uniform(jax.random.fold_in(_gk, 3), (80000,)) ** 2.0).astype(jnp.int32), 19999)
        _o = jnp.argsort(dst, stable=True)
        src = src[_o]
        dst = dst[_o]
        edge_type_8 = jax.random.randint(jax.random.fold_in(_gk, 12), (80000,), 0, 8, jnp.int32)
        return (x, src, dst, edge_type_8)
    x, src, dst, edge_type_8 = _rec_inputs()

    def _L0_gnn_setup():
        import jax, jax.numpy as jnp
        import numpy as np
        N_NODES = 2500
        N_EDGES = 40000
        D = 256
        R = 8

        def _xavier(key, shape):
            fan_in, fan_out = (shape[-2], shape[-1])
            bound = float(np.sqrt(6.0 / (fan_in + fan_out)))
            return jax.random.uniform(key, shape, jnp.float32, -bound, bound)

        def _rgcn_layer(x, W, self_w, b, src, dst, edge_type, num_nodes):
            xW = jnp.einsum('ni,rio->rno', x, W)
            msg = xW[edge_type, src]
            agg = jax.ops.segment_sum(msg, dst, num_segments=num_nodes)
            return agg + x @ self_w + b
        key = jax.random.key(seed)
        ks = jax.random.split(key, 10)
        x = jax.random.normal(ks[0], (N_NODES, D), jnp.float32)
        edge_index = jax.random.randint(ks[1], (2, N_EDGES), 0, N_NODES)
        edge_type = jax.random.randint(ks[2], (N_EDGES,), 0, R)
        W1 = _xavier(ks[3], (R, D, D))
        self_w1 = _xavier(ks[4], (D, D))
        b1 = jnp.zeros((D,), jnp.float32)
        W2 = _xavier(ks[5], (R, D, D))
        self_w2 = _xavier(ks[6], (D, D))
        b2 = jnp.zeros((D,), jnp.float32)
        return {'x': x, 'W1': W1, 'self_w1': self_w1, 'b1': b1, 'W2': W2, 'self_w2': self_w2, 'b2': b2, 'edge_index': edge_index, 'edge_type': edge_type}
    _L0_gnn_all = _L0_gnn_setup()
    _L0_gnn_in = {k: v for k, v in _L0_gnn_all.items() if k in ('W1', 'self_w1', 'b1', 'W2', 'self_w2', 'b2')}
    del _L0_gnn_all
    return {'x': x, 'src': src, 'dst': dst, 'edge_type_8': edge_type_8, 'L0_gnn_W1': _L0_gnn_in['W1'], 'L0_gnn_self_w1': _L0_gnn_in['self_w1'], 'L0_gnn_b1': _L0_gnn_in['b1'], 'L0_gnn_W2': _L0_gnn_in['W2'], 'L0_gnn_self_w2': _L0_gnn_in['self_w2'], 'L0_gnn_b2': _L0_gnn_in['b2']}

def reference(x, src, dst, edge_type_8, L0_gnn_W1, L0_gnn_self_w1, L0_gnn_b1, L0_gnn_W2, L0_gnn_self_w2, L0_gnn_b2):
    import jax
    import jax.numpy as jnp

    def _L0_gnn_ref(x, W1, self_w1, b1, W2, self_w2, b2, edge_index, edge_type):
        import jax, jax.numpy as jnp
        import numpy as np
        N_NODES = 2500
        N_EDGES = 40000
        D = 256
        R = 8

        def _xavier(key, shape):
            fan_in, fan_out = (shape[-2], shape[-1])
            bound = float(np.sqrt(6.0 / (fan_in + fan_out)))
            return jax.random.uniform(key, shape, jnp.float32, -bound, bound)

        def _rgcn_layer(x, W, self_w, b, src, dst, edge_type, num_nodes):
            xW = jnp.einsum('ni,rio->rno', x, W)
            msg = xW[edge_type, src]
            agg = jax.ops.segment_sum(msg, dst, num_segments=num_nodes)
            return agg + x @ self_w + b
        src, dst = (edge_index[0], edge_index[1])
        h = _rgcn_layer(x, W1, self_w1, b1, src, dst, edge_type, N_NODES)
        h = jax.nn.relu(h)
        out = _rgcn_layer(h, W2, self_w2, b2, src, dst, edge_type, N_NODES)
        return out
    edge_index = jnp.stack([src, dst])
    x = _layernorm(x + _L0_gnn_ref(x, L0_gnn_W1, L0_gnn_self_w1, L0_gnn_b1, L0_gnn_W2, L0_gnn_self_w2, L0_gnn_b2, edge_index, edge_type_8), axis=-1)
    return x

_drawn_inputs = setup_inputs


def setup_inputs(seed=0):
    import zlib

    import numpy as np

    out = dict(_drawn_inputs(seed))
    spreads = {'L0_gnn_b1': (0.0, 0.37), 'L0_gnn_b2': (0.0, 0.8)}
    factors = {}
    for name, (base, spread) in spreads.items():
        noise = np.random.default_rng([zlib.crc32(name.encode()), seed]).standard_normal(out[name].shape)
        drawn = base * np.exp(spread * noise) if base else spread * noise
        out[name] = jnp.asarray(drawn.astype(out[name].dtype))
    for name, factor in factors.items():
        out[name] = (out[name] * factor).astype(out[name].dtype)
    return out
```

```python
from contextlib import ExitStack

import concourse.bass as bass
from concourse import mybir

F32 = mybir.dt.float32
I32 = mybir.dt.int32
U32 = mybir.dt.uint32
ALU = mybir.AluOpType
ACT = mybir.ActivationFunctionType
AX = mybir.AxisListType


def gnn_resnorm(nc, x, src, dst, edge_type, w1, self_w1, b1, w2, self_w2, b2, out):
    N, D = x.shape
    E = src.shape[0]
    R = w1.shape[0]
    P = 128
    HALVES = D // P
    TILES = E // P
    SPAN = P // R
    COLS = SPAN * R
    NODES = 125
    NT = N // NODES
    NC = NODES * R
    LP = 125
    LT = TILES // LP
    RING = 12
    BODY = 2 * RING
    LOOPS = TILES // BODY
    REST = TILES - LOOPS * BODY
    LISTED = TILES - REST + RING
    OH = 4
    PIECES = 6
    MARGIN = 6
    EPS = 1e-5
    ACC = (N + SPAN) * R
    assert HALVES == 2 and TILES * P == E and NT * NODES == N and LP * LT == TILES
    assert REST == 1 and COLS == P and RING // 2 == PIECES

    with ExitStack() as ctx:
        def sb(name, shape, dt):
            return ctx.enter_context(nc.sbuf_tensor(name, shape, dt))

        def ps(name, shape, dt=F32):
            return ctx.enter_context(nc.psum_tensor(name, shape, dt))

        def sem(name):
            return ctx.enter_context(nc.semaphore(name))

        sums = sb("sums", [P, HALVES, ACC], F32)
        weights = sb("weights", [P, R + 1, HALVES, D], F32)
        rows = sb("rows", [P, RING, D], F32)
        onehot = sb("onehot", [P, OH, COLS], F32)
        packed = sb("packed", [P, HALVES, R, NODES], F32)
        own = sb("own", [NODES, D], F32)
        own_t = sb("own_t", [P, HALVES, NODES], F32)
        result = sb("result", [NODES, D], F32)
        src_col = sb("src_col", [P, LISTED], mybir.dt.uint16)
        key_col = sb("key_col", [P, LISTED], mybir.dt.uint16)
        src_now = sb("src_now", [P, 2, RING], U32)
        key_now = sb("key_now", [P, 2, RING], F32)
        ident = sb("ident", [P, P], F32)
        offset_row = sb("offset_row", [1, TILES + 7], I32)
        bias = sb("bias", [1, D], F32)
        ones = sb("ones", [1, P], F32)
        zero = sb("zero", [P, 1], F32)
        scalars_row = sb("scalars_row", [1, 32], I32)
        shift = sb("shift", [P, 1], F32)
        row_sum = sb("row_sum", [NODES, NT], F32)
        neg_mean = sb("neg_mean", [NODES, NT], F32)
        square_sum = sb("square_sum", [NODES, NT], F32)
        spread = sb("spread", [NODES, NT], F32)

        src_list = rows[0:LP, 0:5, :].rearrange("p a b -> p (a b)")[:, 0:LT * P].bitcast(I32)
        dst_list = rows[0:LP, 3:6, :].rearrange("p a b -> p (a b)")[:, 0:LT * P].bitcast(I32)
        typ_list = rows[0:LP, 6:9, :].rearrange("p a b -> p (a b)")[:, 0:LT * P].bitcast(I32)
        src_f = rows[0:LP, 9:12, :].rearrange("p a b -> p (a b)")[:, 0:LT * P]
        scratch = packed.rearrange("p a b c -> p (a b c)")
        key_f = scratch[0:LP, 0:LT * P]
        least = scratch[0:LP, 640:645]
        most = scratch[0:LP, 648:653]
        offset_f = scratch[0:LP, 656:661].bitcast(I32)
        width = scratch[0:LP, 664:669]
        widest = scratch[0:LP, 672:673]
        limit = scratch[0:NT, 680:681]
        last_f = scratch[0:NT, 681:682]
        tile_no = scratch[0:NT, 704:704 + TILES]
        offsets_nt = scratch[0:NT, 1332:1332 + TILES].bitcast(I32)
        reach = rows[0:NT, 0:3, :].rearrange("p a b -> p (a b)")[:, 0:TILES]

        banks = [ps(f"bank{i}", [P, 512]) for i in range(OH + 4)]
        product = [banks[i][:, 0:D].rearrange("p (h c) -> p h c", h=HALVES) for i in range(OH)]
        ps_out = banks[OH][0:NODES, 0:D]
        ps_own = banks[OH + 1][:, 0:HALVES * NODES].rearrange("p (h c) -> p h c", h=HALVES)
        ps_iota = banks[OH + 2][:, 0:COLS]
        ps_widest = banks[OH + 3][0:1, 0:LP]
        ps_last = banks[OH][0:1, 0:NT]

        hidden = nc.dram_tensor("hidden", (N, D), F32).ap()
        offset_dram = nc.dram_tensor("offset_dram", (1, TILES), I32).ap()

        s_lists = sem("s_lists")
        s_small = sem("s_small")
        s_const = sem("s_const")
        s_prep = sem("s_prep")
        s_prep_mm = sem("s_prep_mm")
        s_prep_out = sem("s_prep_out")
        s_off_st = sem("s_off_st")
        s_off_ld = sem("s_off_ld")
        s_last = sem("s_last")
        s_tables = sem("s_tables")
        s_tables_end = sem("s_tables_end")
        s_scalars = sem("s_scalars")
        s_iota = sem("s_iota")
        s_iota_ps = sem("s_iota_ps")
        s_zero = sem("s_zero")
        s_reach = sem("s_reach")
        cleared_here = sem("cleared_here")
        staged = sem("staged")
        keyed = sem("keyed")
        landed = [sem(f"landed{j}") for j in range(RING)]
        hot = sem("hot")
        multiplied = sem("multiplied")
        added = sem("added")
        weights_in = sem("weights_in")
        own_in = sem("own_in")
        residual_in = sem("residual_in")
        own_turned = sem("own_turned")
        own_t_ready = sem("own_t_ready")
        packed_ready = sem("packed_ready")
        cleared = sem("cleared")
        transformed = sem("transformed")
        result_ready = sem("result_ready")
        hidden_out = sem("hidden_out")
        stat = sem("stat")
        x_staged = sem("x_staged")
        x_landed = sem("x_landed")
        x_hot = sem("x_hot")
        x_multiplied = sem("x_multiplied")
        x_dve = sem("x_dve")
        s_var = sem("s_var")
        s_sd = sem("s_sd")
        s_rstd = sem("s_rstd")
        s_norm_a = sem("s_norm_a")
        s_norm_v = sem("s_norm_v")
        s_out = sem("s_out")

        block = ctx.enter_context(nc.Block())

        LAST, PASSES = 0, NT
        M0, A0 = RING, OH
        F0 = 1

        def rows_before(layer, j):
            return layer * (LOOPS * 2 + (1 if j < REST else 0)) * 16

        @block.sync
        def _(sp):
            sp.nop().then_inc(hidden_out, 16 * F0)
            sp.dma_start(dst_list, dst.rearrange("(p e) -> p e", p=LP)).then_inc(s_lists, 16)
            sp.dma_start(src_list, src.rearrange("(p e) -> p e", p=LP)).then_inc(s_lists, 16)
            sp.dma_start(typ_list, edge_type.rearrange("(p e) -> p e", p=LP)).then_inc(s_lists, 16)
            sp.wait_ge(s_prep, 2)
            sp.dma_start(offset_dram.rearrange("a (p t) -> (a p) t", p=LP), offset_f).then_inc(s_off_st, 16)
            sp.wait_ge(s_off_st, 16)
            sp.dma_start(offset_row[:, 0:TILES], offset_dram).then_inc(s_off_ld, 16)
            sp.dma_start(offsets_nt, offset_dram.broadcast_to((NT, TILES))).then_inc(s_off_ld, 16)
            for layer, (w, sw, b, table) in enumerate(((w1, self_w1, b1, x), (w2, self_w2, b2, hidden))):
                if layer:
                    sp.wait_ge(transformed, F0 + layer * NT)
                for r in range(R):
                    sp.dma_start(weights[:, r, :, :], w[r].rearrange("(h p) o -> p h o", p=P)).then_inc(weights_in, 16)
                sp.dma_start(weights[:, R, :, :], sw.rearrange("(h p) o -> p h o", p=P)).then_inc(weights_in, 16)
                sp.dma_start(bias[:, :], b.rearrange("(a o) -> a o", a=1)).then_inc(weights_in, 16)
                if layer:
                    sp.wait_ge(hidden_out, 16 * (F0 + NT))
                with sp.Fori(0, NT) as n:
                    sp.wait_ge(transformed, n + (F0 + layer * NT))
                    sp.dma_start(own[:, :], table[bass.ds(n * NODES, NODES), :]).then_inc(own_in, 16)
                    if layer == 1:
                        sp.dma_start(result[:, :], x[bass.ds(n * NODES, NODES), :]).then_inc(residual_in, 16)
                    if layer == 0:
                        sp.wait_ge(result_ready, n + (F0 + 1))
                        sp.dma_start(hidden[bass.ds(n * NODES, NODES), :], result[:, :]).then_inc(hidden_out, 16)
            normal = sums[:, 0, 0:N * R].rearrange("p (n c) -> p n c", n=NT)[:, :, 0:D]
            out_v = out.rearrange("(n p) d -> p n d", p=NODES)
            cut = NODES // 16 * 16
            for half, done in ((0, s_norm_v), (1, s_norm_a)):
                sp.wait_ge(done, NT // 2)
                a, z = half * NT // 2, (half + 1) * NT // 2
                sp.dma_start(out_v[0:cut, a:z, :], normal[0:cut, a:z, :]).then_inc(s_out, 16)
                sp.dma_start(out_v[cut:NODES, a:z, :], normal[cut:NODES, a:z, :]).then_inc(s_out, 16)
            sp.wait_ge(s_out, 64)

        @block.gpsimd
        def _(pool):
            pool.memset(ident[:, :], 0.0).then_inc(s_const, 1)
            pool.wait_ge(s_const, 1)
            pool.affine_select(out=ident[:, :], in_=ident[:, :], compare_op=ALU.not_equal, fill=1.0,
                               base=0, pattern=[[-1, P]], channel_multiplier=1).then_inc(s_const, 1)
            pool.iota(onehot[:, 0, :], [[1, COLS]], base=0, channel_multiplier=0,
                      allow_small_or_imprecise_dtypes=True).then_inc(s_iota, 1)
            pool.iota(tile_no, [[1, TILES]], base=1, channel_multiplier=0,
                      allow_small_or_imprecise_dtypes=True).then_inc(s_last, 1)
            pool.iota(limit, [[1, 1]], base=NC, channel_multiplier=NC,
                      allow_small_or_imprecise_dtypes=True).then_inc(s_last, 1)

            def gather(table, buf, index):
                return pool.indirect_dma_start(out=rows[:, buf, :], out_offset=None, in_=table,
                                               in_offset=bass.IndirectOffsetOnAxis(ap=index, axis=0))

            pool.wait_ge(s_scalars, 2)
            passes = pool.value_load(scalars_row[0:1, PASSES:PASSES + 1], min_val=0, max_val=N // SPAN + 1)
            need = pool.alloc_register("need")
            for layer, table in enumerate((x, hidden)):
                if layer:
                    pool.wait_ge(hidden_out, 16 * (F0 + NT))
                with pool.If(passes > 0):
                    with pool.Fori(0, passes):
                        with pool.Fori(0, TILES):
                            pool.wait_ge(x_staged, 1)
                            pool.sem_clear(x_staged)
                            gather(table, 0, src_now[:, 0, 0:1]).then_inc(x_landed, 16)
                with pool.Fori(0, LOOPS) as c:
                    for j in range(BODY):
                        if j % RING == 0:
                            pool.wait_ge(staged, 2 * c + (layer * (2 * LOOPS + 1) + j // RING + 1))
                        pool.reg_mov(need, BODY * c + (M0 + layer * TILES + j - RING + 1))
                        pool.wait_ge(s_scalars, 2)
                        pool.wait_ge(multiplied, need)
                        gather(table, j % RING, src_now[:, j // RING, j % RING:j % RING + 1]).then_inc(landed[j % RING], 16)
                pool.wait_ge(staged, (layer + 1) * (2 * LOOPS + 1))
                pool.wait_ge(multiplied, M0 + layer * TILES + TILES - RING)
                gather(table, 0, src_now[:, 0, 0:1]).then_inc(landed[0], 16)

        @block.tensor
        def _(pe):
            pe.nop().then_inc(multiplied, M0)
            pe.nop().then_inc(transformed, F0)
            pe.wait_ge(s_const, 2)
            for k, lst in enumerate((key_f, src_f)):
                pe.wait_ge(s_prep, 3 + k)
                for i in range(LT):
                    g = LT * k + i
                    if g >= OH:
                        pe.wait_ge(s_tables, g - OH + 1)
                    pe.transpose(banks[g % OH][:, 0:LP], lst[:, i * P:(i + 1) * P],
                                 ident[0:LP, 0:LP]).then_inc(s_prep_mm, 1)
            pe.wait_ge(s_prep, 5)
            pe.transpose(ps_widest, widest, ident[0:LP, 0:LP]).then_inc(s_prep_mm, 1)
            pe.wait_ge(s_prep, 7)
            pe.transpose(ps_last, last_f, ident[0:NT, 0:NT]).then_inc(s_prep_mm, 1)

            pe.wait_ge(s_scalars, 2)
            passes = pe.value_load(scalars_row[0:1, PASSES:PASSES + 1], min_val=0, max_val=N // SPAN + 1)
            node = pe.alloc_register("node")
            last = pe.alloc_register("last")

            def piece(layer, k):
                n = pe.snap(node, min_val=0, max_val=NT - 1)
                if k == 0:
                    if layer == 0:
                        pe.wait_ge(weights_in, 16 * (R + 2))
                    else:
                        pe.wait_ge(weights_in, 32 * (R + 2))
                    pe.wait_ge(own_in, 16 * n + 16 * (layer * NT + 1))
                    for h in range(HALVES):
                        mm = pe.transpose(ps_own[:, h, :], own[:, h * P:(h + 1) * P], ident[0:NODES, 0:NODES])
                    mm.then_inc(own_turned, 1)
                    pe.wait_ge(result_ready, n + (F0 + layer * NT))
                    pe.matmul(ps_out[:, :], ones[0:1, 0:NODES], bias[:, :], start=True, stop=False)
                    pe.wait_ge(packed_ready, n + (layer * NT + 1))
                parts = [(h, r) for r in range(R) for h in range(HALVES)]
                cuts = [0, 1, 4, 7, 10, 13, 16]
                for h, r in parts[cuts[k]:cuts[k + 1]]:
                    pe.matmul(ps_out[:, :], packed[:, h, r, :], weights[:, r, h, :], start=False, stop=False)
                if k == PIECES - 1:
                    if layer:
                        pe.wait_ge(residual_in, 16 * n + 16)
                        pe.matmul(ps_out[:, :], ident[0:NODES, 0:NODES], result[:, :], start=False, stop=False)
                    pe.wait_ge(own_t_ready, n + (layer * NT + 1))
                    for h in range(HALVES):
                        mm = pe.matmul(ps_out[:, :], own_t[:, h, :], weights[:, R, h, :],
                                       start=False, stop=(h == HALVES - 1))
                    mm.then_inc(transformed, 1)

            def multiply(layer, t, buf, oh, hot_need, landed_need, added_need):
                pe.wait_ge(hot, hot_need)
                pe.wait_ge(landed[buf], landed_need)
                pe.wait_ge(added, added_need)
                for h in range(HALVES):
                    mm = pe.matmul(product[oh][:, h, :], rows[:, buf, h * P:(h + 1) * P], onehot[:, oh, :],
                                   start=True, stop=True)
                mm.then_inc(multiplied, 1)

            for layer in range(2):
                with pe.If(passes > 0):
                    with pe.Fori(0, passes):
                        with pe.Fori(0, TILES):
                            pe.wait_ge(x_hot, 1)
                            pe.sem_clear(x_hot)
                            pe.wait_ge(x_landed, 16)
                            pe.sem_clear(x_landed)
                            for h in range(HALVES):
                                mm = pe.matmul(product[0][:, h, :], rows[:, 0, h * P:(h + 1) * P],
                                               onehot[:, 0, :], start=True, stop=True)
                            mm.then_inc(x_multiplied, 1)
                pe.reg_mov(node, 0)
                pe.reg_load(last, scalars_row[0:1, LAST:LAST + 1])
                with pe.Fori(0, LOOPS) as c:
                    for j in range(BODY):
                        t0 = layer * TILES + j
                        multiply(layer, None, j % RING, j % OH,
                                 BODY * c + (t0 + 1),
                                 32 * c + (rows_before(layer, j % RING) + 16 * (j // RING + 1)),
                                 BODY * c + (A0 + t0 + 1 - OH))
                        if j % 2 == 1:
                            q, k = j // RING, (j % RING) // 2
                            done = BODY * c + RING * q
                            with pe.If(pe.snap(last, min_val=0, max_val=TILES) + MARGIN <= done):
                                piece(layer, k)
                                if k == PIECES - 1:
                                    pe.reg_add(node, node, 1)
                                    pe.reg_load(last, scalars_row[0:1, bass.ds(pe.snap(node, min_val=0, max_val=NT - 1), 1)])
                multiply(layer, None, 0, (LOOPS * BODY) % OH, (layer + 1) * TILES,
                         rows_before(layer + 1, 0), A0 + (layer + 1) * TILES - OH)
                with pe.Fori(pe.snap(node, min_val=0, max_val=NT - 1), NT) as m:
                    pe.reg_mov(node, m)
                    for k in range(PIECES):
                        piece(layer, k)

        @block.scalar
        def _(act):
            act.nop().then_inc(result_ready, F0)
            act.wait_ge(s_zero, 1)
            act.activation(sums[:, 0, :], zero[:, 0:1].broadcast_to((P, ACC)), ACT.Copy).then_inc(cleared, 1)
            act.wait_ge(s_scalars, 2)
            need = act.alloc_register("need")
            for layer in range(2):
                with act.Fori(0, NT) as n:
                    final = act.value_load(scalars_row[0:1, bass.ds(n, 1)], min_val=0, max_val=TILES)
                    act.reg_mov(need, final + (A0 + layer * TILES))
                    act.wait_ge(s_scalars, 2)
                    act.wait_ge(added, need)
                    act.wait_ge(transformed, n + (F0 + layer * NT))
                    act.activation(packed[:, :, :, :],
                                   sums[:, :, bass.ds(n * NC, NC)].rearrange("p h (m r) -> p h r m", r=R),
                                   ACT.Copy).then_inc(packed_ready, 1)
                    if layer == 0:
                        act.reg_mov(need, n + 1)
                        act.wait_ge(s_scalars, 2)
                        act.wait_ge(packed_ready, need)
                        act.activation(sums[:, :, bass.ds(n * NC, NC)],
                                       zero[:, None, 0:1].broadcast_to((P, HALVES, NC)), ACT.Copy).then_inc(cleared, 1)
                    act.wait_ge(own_turned, n + (layer * NT + 1))
                    act.activation(own_t[:, :, :], ps_own[:, :, :], ACT.Copy).then_inc(own_t_ready, 1)
                    act.reg_mov(need, n + (F0 + layer * NT + 1))
                    act.wait_ge(s_scalars, 2)
                    act.wait_ge(transformed, need)
                    if layer == 0:
                        act.wait_ge(hidden_out, 16 * n + 16 * F0)
                        act.activation(result[:, :], ps_out[:, :], ACT.Relu).then_inc(result_ready, 1)
                    else:
                        act.activation(sums[0:NODES, 0, bass.ds(n * NC, D)], ps_out[:, :], ACT.Identity,
                                       accum_out=row_sum[:, bass.ds(n, 1)]).then_inc(stat, 1)
                        act.reg_mov(need, 2 * n + 1)
                        act.wait_ge(s_scalars, 2)
                        act.wait_ge(stat, need)
                        act.activation(neg_mean[:, bass.ds(n, 1)], row_sum[:, bass.ds(n, 1)], ACT.Copy,
                                       scale=-1.0 / D).then_inc(stat, 1)
                        act.reg_mov(need, 2 * n + 2)
                        act.wait_ge(s_scalars, 2)
                        act.wait_ge(stat, need)
                        act.activation(ps_out[:, :], ps_out[:, :], ACT.Square, bias=neg_mean[:, bass.ds(n, 1)],
                                       accum_out=square_sum[:, bass.ds(n, 1)]).then_inc(result_ready, 1)
            act.wait_ge(s_var, 1)
            act.activation(spread[:, :], spread[:, :], ACT.Sqrt).then_inc(s_sd, 1)
            act.wait_ge(s_rstd, 2)
            for n in range(NT // 2, NT):
                y = sums[0:NODES, 0, n * NC:n * NC + D]
                act.activation(y, y, ACT.Identity, bias=row_sum[:, n:n + 1],
                               scale=spread[:, n:n + 1]).then_inc(s_norm_a, 1)

        @block.vector
        def _(dve):
            dve.memset(zero[:, :], 0.0).then_inc(s_zero, 1)
            dve.memset(ones[:, :], 1.0).then_inc(added, A0)
            dve.memset(src_col[:, TILES:LISTED], 0).then_inc(s_tables_end, 1)
            dve.memset(key_col[:, TILES:LISTED], 0).then_inc(s_tables_end, 1)
            dve.wait_ge(s_lists, 48)
            lists = dst_list.rearrange("p (t e) -> p t e", t=LT)
            dve.tensor_reduce(least, lists, AX.X, ALU.min).then_inc(s_prep, 1)
            dve.wait_ge(s_prep, 1)
            dve.tensor_scalar(offset_f, least, float(R), None, ALU.mult).then_inc(s_prep, 1)
            for i in range(LT):
                e = slice(i * P, (i + 1) * P)
                op = dve.tensor_scalar(key_f[:, e], dst_list[:, e], least[:, i:i + 1], float(R), ALU.subtract, ALU.mult)
            op.then_inc(s_prep_out, 1)
            dve.wait_ge(s_prep_out, 1)
            dve.tensor_tensor(key_f, key_f, typ_list, ALU.add).then_inc(s_prep, 1)
            dve.tensor_copy(src_f, src_list).then_inc(s_prep, 1)
            dve.tensor_reduce(most, lists, AX.X, ALU.max).then_inc(s_prep_out, 1)
            dve.wait_ge(s_prep_out, 2)
            dve.tensor_tensor(width, most, least, ALU.subtract).then_inc(s_prep_out, 1)
            dve.wait_ge(s_prep_out, 3)
            dve.tensor_reduce(widest, width, AX.X, ALU.max).then_inc(s_prep, 1)
            for k, table in enumerate((key_col, src_col)):
                cols = table[:, 0:TILES].rearrange("p (q i) -> p i q", i=LT)
                for i in range(LT):
                    g = LT * k + i
                    dve.wait_ge(s_prep_mm, g + 1)
                    dve.tensor_copy(cols[:, i, :], banks[g % OH][:, 0:LP]).then_inc(s_tables, 1)
            dve.wait_ge(s_iota, 1)
            dve.tensor_copy(ps_iota[:, :], onehot[:, 0, :]).then_inc(s_iota_ps, 1)
            dve.wait_ge(s_prep_mm, 2 * LT + 1)
            dve.tensor_reduce(scalars_row[0:1, PASSES + 1:PASSES + 2], ps_widest, AX.X,
                              ALU.max).then_inc(s_prep, 1)
            dve.wait_ge(s_prep, 6)
            dve.tensor_scalar(scalars_row[0:1, PASSES:PASSES + 1], scalars_row[0:1, PASSES + 1:PASSES + 2],
                              SPAN.bit_length() - 1, None, ALU.logical_shift_right).then_inc(s_scalars, 1)
            dve.wait_ge(s_off_ld, 32)
            dve.wait_ge(s_last, 2)
            dve.scalar_tensor_tensor(out=reach, in0=offsets_nt, scalar=limit, in1=tile_no,
                                     op0=ALU.is_lt, op1=ALU.mult).then_inc(s_reach, 1)
            dve.wait_ge(s_reach, 1)
            dve.tensor_reduce(last_f, reach, AX.X, ALU.max).then_inc(s_prep, 1)
            dve.wait_ge(s_prep_mm, 2 * LT + 2)
            dve.tensor_copy(scalars_row[0:1, LAST:LAST + NT], ps_last).then_inc(s_scalars, 1)
            dve.memset(sums[:, 1, :], 0.0).then_inc(cleared_here, 1)
            dve.wait_ge(s_tables, 2 * LT)
            dve.wait_ge(s_tables_end, 2)
            dve.wait_ge(s_iota_ps, 1)
            dve.wait_ge(s_scalars, 2)
            passes = dve.value_load(scalars_row[0:1, PASSES:PASSES + 1], min_val=0, max_val=N // SPAN + 1)

            def stage(column, buf):
                dve.tensor_copy(src_now[:, buf, :], src_col[:, bass.ds(column, RING)]).then_inc(staged, 1)
                dve.tensor_copy(key_now[:, buf, :], key_col[:, bass.ds(column, RING)]).then_inc(keyed, 1)

            def make_onehot(oh, key):
                return dve.tensor_scalar(onehot[:, oh, :], ps_iota[:, :], key, None, ALU.is_equal)

            def add(product_buf, offset):
                part = sums[:, :, bass.ds(offset, COLS)]
                return dve.tensor_tensor(part, part, product[product_buf][:, :, :], ALU.add)

            at = dve.alloc_register("at")
            offs = [dve.alloc_register(f"offset{j}") for j in range(BODY)]
            for layer in range(2):
                T0 = layer * TILES
                dve.wait_ge(cleared_here, 1)
                dve.wait_ge(cleared, 1 if layer == 0 else 1 + NT)
                with dve.If(passes > 0):
                    dve.memset(shift[:, :], 0.0).then_inc(x_dve, 1)
                    dve.wait_ge(x_dve, 1)
                    dve.sem_clear(x_dve)
                    with dve.Fori(0, passes) as p:
                        dve.tensor_scalar(shift[:, :], shift[:, :], float(COLS), None, ALU.add).then_inc(x_dve, 1)
                        dve.wait_ge(x_dve, 1)
                        dve.sem_clear(x_dve)
                        with dve.Fori(0, TILES) as t:
                            dve.tensor_copy(src_now[:, 0, 0:1], src_col[:, bass.ds(t, 1)]).then_inc(x_staged, 1)
                            dve.tensor_copy(key_now[:, 0, 0:1], key_col[:, bass.ds(t, 1)]).then_inc(x_dve, 1)
                            dve.wait_ge(x_dve, 1)
                            dve.sem_clear(x_dve)
                            dve.tensor_scalar(onehot[:, 0, :], ps_iota[:, :], shift[:, 0:1], key_now[:, 0, 0:1],
                                              ALU.add, ALU.is_equal).then_inc(x_hot, 1)
                            base = dve.value_load(offset_row[0:1, bass.ds(t, 1)], min_val=0, max_val=N * R)
                            dve.reg_alu(at, dve.to_reg(base + (p + 1) * COLS), N * R, ALU.min)
                            dve.wait_ge(x_multiplied, 1)
                            dve.sem_clear(x_multiplied)
                            add(0, dve.snap(at, min_val=0, max_val=N * R)).then_inc(x_dve, 1)
                            dve.wait_ge(x_dve, 1)
                            dve.sem_clear(x_dve)
                stage(0, 0)
                with dve.Fori(0, LOOPS) as c:
                    dve.reg_load(offs, offset_row[0:1, bass.ds(c * BODY, BODY)])
                    for j in range(BODY + 2):
                        if j < BODY:
                            if j == 0:
                                stage(c * BODY + RING, 1)
                            if j % RING == 0:
                                dve.wait_ge(keyed, 2 * c + (layer * (2 * LOOPS + 1) + j // RING + 1))
                            dve.wait_ge(multiplied, BODY * c + (M0 + T0 + j - OH + 1))
                            make_onehot(j % OH, key_now[:, j // RING, j % RING:j % RING + 1]).then_inc(hot, 1)
                        if j >= 2:
                            i = j - 2
                            dve.wait_ge(multiplied, BODY * c + (M0 + T0 + i + 1))
                            dve.wait_ge(added, BODY * c + (A0 + T0 + i))
                            add(i % OH, dve.snap(offs[i], min_val=0, max_val=N * R)).then_inc(added, 1)
                            if i == RING - 1:
                                stage(c * BODY + BODY, 0)
                dve.wait_ge(keyed, (layer + 1) * (2 * LOOPS + 1))
                make_onehot((TILES - 1) % OH, key_now[:, 0, 0:1]).then_inc(hot, 1)
                last_offset = dve.value_load(offset_row[0:1, TILES - 1:TILES], min_val=0, max_val=N * R)
                dve.wait_ge(multiplied, M0 + T0 + TILES)
                dve.wait_ge(added, A0 + T0 + TILES - 1)
                add((TILES - 1) % OH, last_offset).then_inc(added, 1)

            dve.wait_ge(result_ready, F0 + 2 * NT)
            dve.tensor_scalar(spread[:, :], square_sum[:, :], 1.0 / D, EPS, ALU.mult, ALU.add).then_inc(s_var, 1)
            dve.wait_ge(s_sd, 1)
            dve.reciprocal(spread[:, :], spread[:, :]).then_inc(s_rstd, 1)
            dve.wait_ge(s_rstd, 1)
            dve.tensor_tensor(row_sum[:, :], neg_mean[:, :], spread[:, :], ALU.mult).then_inc(s_rstd, 1)
            for n in range(NT // 2):
                y = sums[0:NODES, 0, n * NC:n * NC + D]
                dve.tensor_scalar(y, y, neg_mean[:, n:n + 1], spread[:, n:n + 1], ALU.add,
                                  ALU.mult).then_inc(s_norm_v, 1)


_INS = ['x', 'src', 'dst', 'edge_type_8', 'L0_gnn_W1', 'L0_gnn_self_w1', 'L0_gnn_b1', 'L0_gnn_W2', 'L0_gnn_self_w2', 'L0_gnn_b2']


def kernel(**inputs):
    import numpy as _np
    import concourse.bacc as _bacc
    from concourse import mybir as _mybir
    from concourse.bass_utils import run_bass_kernel_spmd as _run

    nc = _bacc.Bacc("TRN2", target_bir_lowering=False, num_devices=1)
    arrays, args = {}, []
    for name in _INS:
        a = _np.ascontiguousarray(inputs[name])
        arrays[f"in_{name}_dram"] = a
        args.append(nc.dram_tensor(f"in_{name}_dram", a.shape, _mybir.dt.from_np(a.dtype), kind="ExternalInput").ap())
    args.append(nc.dram_tensor("out_dram", tuple(inputs['x'].shape), _mybir.dt.float32, kind="ExternalOutput").ap())
    gnn_resnorm(nc, *args)
    r = _run(nc, [arrays], core_ids=[0])
    return r.results[0]["out_dram"]
```

```python
from contextlib import ExitStack

import concourse.bass as bass
from concourse import mybir

F32 = mybir.dt.float32
I32 = mybir.dt.int32
U32 = mybir.dt.uint32
ALU = mybir.AluOpType
ACT = mybir.ActivationFunctionType
AX = mybir.AxisListType


def gnn_resnorm(nc, x, src, dst, edge_type, w1, self_w1, b1, w2, self_w2, b2, out):
    N, D = x.shape
    E = src.shape[0]
    R = w1.shape[0]
    P = 128
    HALVES = D // P
    TILES = E // P
    SPAN = 12
    COLS = SPAN * R
    NODES = 125
    NT = N // NODES
    NC = NODES * R
    LP = 125
    LT = TILES // LP
    RING = 13
    BODY = 4 * RING
    LOOPS = TILES // BODY
    REST = TILES - LOOPS * BODY
    STAGINGS = LOOPS * BODY // RING + 1
    LISTED = TILES - REST + RING
    LOAD = 16
    OH = 4
    PIECES = 6
    EPS = 1e-5
    ACC = (N + SPAN) * R
    assert HALVES == 2 and TILES * P == E and NT * NODES == N and LP * LT == TILES
    assert REST == 1 and COLS <= P and RING // 2 == PIECES

    with ExitStack() as ctx:
        def sb(name, shape, dt):
            return ctx.enter_context(nc.sbuf_tensor(name, shape, dt))

        def ps(name, shape, dt=F32):
            return ctx.enter_context(nc.psum_tensor(name, shape, dt))

        def sem(name):
            return ctx.enter_context(nc.semaphore(name))

        sums = sb("sums", [P, HALVES, ACC], F32)
        weights = sb("weights", [P, R + 1, HALVES, D], F32)
        rows = sb("rows", [P, RING, D], F32)
        onehot = sb("onehot", [P, OH, COLS], F32)
        packed = sb("packed", [P, HALVES, R, NODES], F32)
        own = sb("own", [NODES, D], F32)
        own_t = sb("own_t", [P, HALVES, NODES], F32)
        result = sb("result", [NODES, D], F32)
        src_col = sb("src_col", [P, LISTED], mybir.dt.uint16)
        key_col = sb("key_col", [P, LISTED], mybir.dt.uint16)
        src_now = sb("src_now", [P, 2, RING], U32)
        key_now = sb("key_now", [P, 2, RING], F32)
        ident = sb("ident", [P, P], F32)
        single = sb("single", [33, TILES + 7], F32)
        offset_row = single[0:1, :].bitcast(I32)
        bias = single[32:33, 0:D]
        ones = single[32:33, D:D + P]
        zero = sb("zero", [P, 1], F32)
        scalars_row = sb("scalars_row", [1, 32], I32)
        shift = sb("shift", [P, 1], F32)
        row_sum = sb("row_sum", [NODES, NT], F32)
        neg_mean = sb("neg_mean", [NODES, NT], F32)
        square_sum = sb("square_sum", [NODES, NT], F32)
        spread = square_sum

        prep = weights.rearrange("p a b c -> p (a b c)")
        L = LT * P
        dst_list, src_list, typ_list = (prep[0:LP, i * L:(i + 1) * L].bitcast(I32) for i in range(3))
        src_f, key_f = (prep[0:LP, i * L:(i + 1) * L] for i in range(3, 5))
        tile_no = prep[0:NT, 5 * L:5 * L + TILES]
        offsets_nt = prep[0:NT, 5 * L + TILES:5 * L + 2 * TILES].bitcast(I32)
        at = 5 * L + 2 * TILES
        least, most, width = (prep[0:LP, at + i * LT:at + (i + 1) * LT] for i in range(3))
        offset_f = prep[0:LP, at + 3 * LT:at + 4 * LT].bitcast(I32)
        widest = prep[0:LP, at + 4 * LT:at + 4 * LT + 1]
        limit = prep[0:NT, at + 4 * LT + 1:at + 4 * LT + 2]
        last_f = prep[0:NT, at + 4 * LT + 2:at + 4 * LT + 3]

        banks = [ps(f"bank{i}", [P, 512]) for i in range(OH + 4)]
        product = [banks[i][:, 0:HALVES * COLS].rearrange("p (h c) -> p h c", h=HALVES) for i in range(OH)]
        ps_out = banks[OH][0:NODES, 0:D]
        ps_own = banks[OH + 1][:, 0:HALVES * NODES].rearrange("p (h c) -> p h c", h=HALVES)
        ps_iota = banks[OH + 2][:, 0:COLS]
        ps_widest = banks[OH + 3][0:1, 0:LP]
        ps_last = banks[OH][0:1, 0:NT]

        hidden = nc.dram_tensor("hidden", (N, D), F32).ap()
        offset_dram = nc.dram_tensor("offset_dram", (1, TILES), I32).ap()

        s_dst = sem("s_dst")
        s_src = sem("s_src")
        s_typ = sem("s_typ")
        s_const = sem("s_const")
        s_zero = sem("s_zero")
        s_iota = sem("s_iota")
        s_iota_ps = sem("s_iota_ps")
        s_ends = sem("s_ends")
        s_block = sem("s_block")
        s_stats = sem("s_stats")
        s_offset = sem("s_offset")
        s_off_st = sem("s_off_st")
        s_off_ld = sem("s_off_ld")
        s_widest = sem("s_widest")
        s_widest_t = sem("s_widest_t")
        s_width = sem("s_width")
        s_list_f = sem("s_list_f")
        s_turned = sem("s_turned")
        s_tables = sem("s_tables")
        s_limits = sem("s_limits")
        s_reach = sem("s_reach")
        s_last_f = sem("s_last_f")
        s_last_t = sem("s_last_t")
        s_last_row = sem("s_last_row")
        staged = sem("staged")
        keyed = sem("keyed")
        landed = [sem(f"landed{j}") for j in range(RING)]
        hot = sem("hot")
        multiplied = sem("multiplied")
        added = sem("added")
        weights_in = sem("weights_in")
        own_in = sem("own_in")
        residual_in = sem("residual_in")
        own_turned = sem("own_turned")
        own_t_ready = sem("own_t_ready")
        packed_ready = sem("packed_ready")
        cleared = sem("cleared")
        cleared_pool = sem("cleared_pool")
        cleared_dve = sem("cleared_dve")
        cleared_dma = sem("cleared_dma")
        transformed = sem("transformed")
        result_ready = sem("result_ready")
        hidden_out = sem("hidden_out")
        stat = sem("stat")
        x_staged = sem("x_staged")
        x_landed = sem("x_landed")
        x_hot = sem("x_hot")
        x_multiplied = sem("x_multiplied")
        x_dve = sem("x_dve")
        s_var = sem("s_var")
        s_sd = sem("s_sd")
        s_rstd = sem("s_rstd")
        s_norm_a = sem("s_norm_a")
        s_norm_v = sem("s_norm_v")
        s_out = sem("s_out")

        block = ctx.enter_context(nc.Block())

        LAST, WIDTH = 0, NT
        FIRST = 11
        CLEAR_BLOCK = 2400
        CLEAR_DMA = 4 * CLEAR_BLOCK
        CLEAR_POOL = 15400
        M0, A0 = RING, OH
        F0 = 1

        def rows_before(layer, j):
            return layer * (LOOPS * BODY // RING + (1 if j < REST else 0)) * 16

        @block.sync
        def _(sp):
            sp.nop().then_inc(hidden_out, 16 * F0)
            sp.dma_start(dst_list, dst.rearrange("(p e) -> p e", p=LP)).then_inc(s_dst, 16)
            sp.dma_start(src_list, src.rearrange("(p e) -> p e", p=LP)).then_inc(s_src, 16)
            sp.dma_start(typ_list, edge_type.rearrange("(p e) -> p e", p=LP)).then_inc(s_typ, 16)
            sp.wait_ge(s_block, 1)

            def copy_block(i):
                sp.dma_start(sums[:, 1, i:i + CLEAR_BLOCK], sums[:, 1, 0:CLEAR_BLOCK]).then_inc(cleared_dma, 16)

            copy_block(CLEAR_BLOCK)
            sp.wait_ge(s_offset, 1)
            sp.dma_start(offset_dram.rearrange("a (p t) -> (a p) t", p=LP), offset_f).then_inc(s_off_st, 16)
            copy_block(2 * CLEAR_BLOCK)
            sp.wait_ge(s_off_st, 16)
            sp.dma_start(offset_row[:, 0:TILES], offset_dram).then_inc(s_off_ld, 16)
            sp.dma_start(offsets_nt, offset_dram.broadcast_to((NT, TILES))).then_inc(s_off_ld, 16)
            copy_block(3 * CLEAR_BLOCK)
            for layer, (w, sw, b, table) in enumerate(((w1, self_w1, b1, x), (w2, self_w2, b2, hidden))):
                if layer == 0:
                    sp.wait_ge(s_tables, 2 * LT)
                    sp.wait_ge(s_last_row, 1)
                else:
                    sp.wait_ge(transformed, F0 + layer * NT)
                for r in range(R):
                    sp.dma_start(weights[:, r, :, :], w[r].rearrange("(h p) o -> p h o", p=P)).then_inc(weights_in, 16)
                sp.dma_start(weights[:, R, :, :], sw.rearrange("(h p) o -> p h o", p=P)).then_inc(weights_in, 16)
                sp.dma_start(bias[:, :], b.rearrange("(a o) -> a o", a=1)).then_inc(weights_in, 16)
                if layer:
                    sp.wait_ge(hidden_out, 16 * (F0 + NT))

                def load(n):
                    sp.wait_ge(own_turned, n + (F0 + layer * NT))
                    sp.dma_start(own[:, :], table[bass.ds(n * NODES, NODES), :]).then_inc(own_in, 16)
                    if layer == 1:
                        sp.wait_ge(transformed, n + (F0 + NT))
                        sp.dma_start(result[:, :], x[bass.ds(n * NODES, NODES), :]).then_inc(residual_in, 16)

                def store(n):
                    if layer == 0:
                        sp.wait_ge(result_ready, n + (F0 + 1))
                        sp.dma_start(hidden[bass.ds(n * NODES, NODES), :], result[:, :]).then_inc(hidden_out, 16)

                load(0)
                with sp.Fori(0, NT - 1) as n:
                    load(n + 1)
                    store(n)
                store(NT - 1)
            normal = sums[:, 0, 0:N * R].rearrange("p (n c) -> p n c", n=NT)[:, :, 0:D]
            out_v = out.rearrange("(n p) d -> p n d", p=NODES)
            cut = NODES // 16 * 16
            for done, count, a, z in ((s_norm_v, FIRST, 0, FIRST), (s_norm_a, NT - 1 - FIRST, FIRST, NT - 1),
                                      (s_norm_v, FIRST + 1, NT - 1, NT)):
                sp.wait_ge(done, count)
                sp.dma_start(out_v[0:cut, a:z, :], normal[0:cut, a:z, :]).then_inc(s_out, 16)
                sp.dma_start(out_v[cut:NODES, a:z, :], normal[cut:NODES, a:z, :]).then_inc(s_out, 16)
            sp.wait_ge(s_out, 6 * 16)

        @block.gpsimd
        def _(pool):
            pool.memset(ident[:, :], 0.0).then_inc(s_const, 1)
            pool.wait_ge(s_const, 1)
            pool.affine_select(out=ident[:, :], in_=ident[:, :], compare_op=ALU.not_equal, fill=1.0,
                               base=0, pattern=[[-1, P]], channel_multiplier=1).then_inc(s_const, 1)
            pool.iota(onehot[:, 0, :], [[1, COLS]], base=0, channel_multiplier=0,
                      allow_small_or_imprecise_dtypes=True).then_inc(s_iota, 1)
            pool.iota(tile_no, [[1, TILES]], base=1, channel_multiplier=0,
                      allow_small_or_imprecise_dtypes=True).then_inc(s_limits, 1)
            pool.iota(limit, [[1, 1]], base=NC, channel_multiplier=NC,
                      allow_small_or_imprecise_dtypes=True).then_inc(s_limits, 1)
            pool.memset(sums[:, 1, CLEAR_DMA:CLEAR_POOL], 0.0).then_inc(cleared_pool, 1)

            def gather(table, buf, index):
                return pool.indirect_dma_start(out=rows[:, buf, :], out_offset=None, in_=table,
                                               in_offset=bass.IndirectOffsetOnAxis(ap=index, axis=0))

            pool.wait_ge(s_width, 1)
            passes = pool.value_load(scalars_row[0:1, WIDTH:WIDTH + 1], min_val=0, max_val=N) // SPAN
            need = pool.alloc_register("need")
            for layer, table in enumerate((x, hidden)):
                if layer:
                    pool.wait_ge(hidden_out, 16 * (F0 + NT))
                with pool.If(passes > 0):
                    with pool.Fori(0, passes):
                        with pool.Fori(0, TILES):
                            pool.wait_ge(x_staged, 1)
                            pool.sem_clear(x_staged)
                            gather(table, 0, src_now[:, 1, 0:1]).then_inc(x_landed, 16)
                with pool.Fori(0, LOOPS) as c:
                    for j in range(BODY):
                        if j % RING == 0:
                            pool.wait_ge(staged, BODY // RING * c + (layer * STAGINGS + j // RING + 1))
                        pool.reg_mov(need, BODY * c + (M0 + layer * TILES + j - RING + 1))
                        pool.wait_ge(s_width, 1)
                        pool.wait_ge(multiplied, need)
                        gather(table, j % RING, src_now[:, j // RING % 2, j % RING:j % RING + 1]).then_inc(landed[j % RING], 16)
                pool.wait_ge(staged, (layer + 1) * STAGINGS)
                pool.wait_ge(multiplied, M0 + layer * TILES + TILES - RING)
                gather(table, 0, src_now[:, 0, 0:1]).then_inc(landed[0], 16)

        @block.tensor
        def _(pe):
            pe.nop().then_inc(multiplied, M0)
            pe.nop().then_inc(transformed, F0)
            pe.nop().then_inc(own_turned, F0)
            pe.wait_ge(s_const, 2)
            for k, lst in enumerate((src_f, key_f)):
                if k == 0:
                    pe.wait_ge(s_widest, 1)
                    pe.transpose(ps_widest, widest, ident[0:LP, 0:LP]).then_inc(s_widest_t, 1)
                pe.wait_ge(s_list_f, k + 1)
                for i in range(LT):
                    g = LT * k + i
                    if g >= OH:
                        pe.wait_ge(s_tables, g - OH + 1)
                    pe.transpose(banks[g % OH][:, 0:LP], lst[:, i * P:(i + 1) * P],
                                 ident[0:LP, 0:LP]).then_inc(s_turned, 1)
            pe.wait_ge(s_last_f, 1)
            pe.transpose(ps_last, last_f, ident[0:NT, 0:NT]).then_inc(s_last_t, 1)

            pe.wait_ge(s_width, 1)
            passes = pe.value_load(scalars_row[0:1, WIDTH:WIDTH + 1], min_val=0, max_val=N) // SPAN
            pe.wait_ge(s_last_row, 1)
            CUTS = [0, 0, 1, 5, 9, 13, 16]
            node = pe.alloc_register("node")
            last = pe.alloc_register("last")
            gathered = pe.alloc_register("gathered")
            pe.reg_mov(gathered, 0)

            def piece(layer, k):
                n = pe.snap(node, min_val=0, max_val=NT - 1)
                if k == 0:
                    if layer == 0:
                        pe.wait_ge(weights_in, 16 * (R + 2))
                    else:
                        pe.wait_ge(weights_in, 32 * (R + 2))
                    pe.wait_ge(own_in, 16 * n + 16 * (layer * NT + 1))
                    for h in range(HALVES):
                        mm = pe.transpose(ps_own[:, h, :], own[:, h * P:(h + 1) * P], ident[0:NODES, 0:NODES])
                    mm.then_inc(own_turned, 1)
                    pe.wait_ge(result_ready, n + (F0 + layer * NT))
                    pe.matmul(ps_out[:, :], ones[:, 0:NODES], bias[:, :], start=True, stop=False)
                    if layer:
                        pe.wait_ge(residual_in, 16 * n + 16)
                        pe.matmul(ps_out[:, :], ident[0:NODES, 0:NODES], result[:, :], start=False, stop=False)
                if k == 1:
                    pe.wait_ge(own_t_ready, n + (layer * NT + 1))
                    for h in range(HALVES):
                        pe.matmul(ps_out[:, :], own_t[:, h, :], weights[:, R, h, :], start=False, stop=False)
                parts = [(h, r) for h in range(HALVES) for r in range(R)]
                for h, r in parts[CUTS[k]:CUTS[k + 1]]:
                    if r == 0:
                        pe.wait_ge(packed_ready, 2 * n + (2 * layer * NT + h + 1))
                    mm = pe.matmul(ps_out[:, :], packed[:, h, r, :], weights[:, r, h, :],
                                   start=False, stop=(h, r) == parts[-1])
                if k == PIECES - 1:
                    mm.then_inc(transformed, 1)

            def multiply(layer, t, buf, oh, hot_need, landed_need, added_need):
                pe.wait_ge(hot, hot_need)
                pe.wait_ge(landed[buf], landed_need)
                pe.wait_ge(added, added_need)
                for h in range(HALVES):
                    mm = pe.matmul(product[oh][:, h, :], rows[:, buf, h * P:(h + 1) * P], onehot[:, oh, :],
                                   start=True, stop=True)
                mm.then_inc(multiplied, 1)

            for layer in range(2):
                with pe.If(passes > 0):
                    with pe.Fori(0, passes):
                        with pe.Fori(0, TILES):
                            pe.wait_ge(x_hot, 1)
                            pe.sem_clear(x_hot)
                            pe.reg_add(gathered, gathered, 16)
                            pe.wait_ge(x_landed, pe.snap(gathered, min_val=16))
                            for h in range(HALVES):
                                mm = pe.matmul(product[0][:, h, :], rows[:, 0, h * P:(h + 1) * P],
                                               onehot[:, 0, :], start=True, stop=True)
                            mm.then_inc(x_multiplied, 1)
                pe.reg_mov(node, 0)
                pe.reg_load(last, scalars_row[0:1, LAST:LAST + 1])
                with pe.Fori(0, LOOPS) as c:
                    for j in range(BODY):
                        t0 = layer * TILES + j
                        multiply(layer, None, j % RING, j % OH,
                                 BODY * c + (t0 + 1),
                                 16 * BODY // RING * c + (rows_before(layer, j % RING) + 16 * (j // RING + 1)),
                                 BODY * c + (A0 + t0 + 1 - OH))
                        if j % RING % 2 == 1 and j % RING < 2 * PIECES:
                            q, k = j // RING, (j % RING) // 2
                            done = BODY * c + RING * q
                            with pe.If(pe.snap(last, min_val=0, max_val=TILES) <= done):
                                piece(layer, k)
                                if k == PIECES - 1:
                                    pe.reg_add(node, node, 1)
                                    pe.reg_load(last, scalars_row[0:1, bass.ds(pe.snap(node, min_val=0, max_val=NT - 1), 1)])
                multiply(layer, None, 0, (LOOPS * BODY) % OH, (layer + 1) * TILES,
                         rows_before(layer + 1, 0), A0 + (layer + 1) * TILES - OH)
                with pe.Fori(pe.snap(node, min_val=0, max_val=NT - 1), NT) as m:
                    pe.reg_mov(node, m)
                    for k in range(PIECES):
                        piece(layer, k)

        @block.scalar
        def _(act):
            act.nop().then_inc(result_ready, F0)
            act.wait_ge(s_zero, 1)
            act.activation(sums[:, 0, :], zero[:, 0:1].broadcast_to((P, ACC)), ACT.Copy).then_inc(cleared, 1)
            need = act.alloc_register("need")

            def pack(layer, n):
                act.wait_ge(own_turned, n + (F0 + layer * NT + 1))
                act.activation(own_t[:, :, :], ps_own[:, :, :], ACT.Copy).then_inc(own_t_ready, 1)
                final = act.value_load(scalars_row[0:1, bass.ds(n, 1)], min_val=0, max_val=TILES)
                act.reg_mov(need, final + (A0 + layer * TILES))
                act.wait_ge(s_zero, 1)
                act.wait_ge(added, need)
                for h in range(HALVES):
                    act.activation(packed[:, h, :, :],
                                   sums[:, h, bass.ds(n * NC, NC)].rearrange("p (m r) -> p r m", r=R),
                                   ACT.Copy).then_inc(packed_ready, 1)
                if layer == 0:
                    act.reg_mov(need, 2 * n + 2)
                    act.wait_ge(s_zero, 1)
                    act.wait_ge(packed_ready, need)
                    act.activation(sums[:, :, bass.ds(n * NC, NC)],
                                   zero[:, None, 0:1].broadcast_to((P, HALVES, NC)), ACT.Copy).then_inc(cleared, 1)

            def finish(layer, n):
                act.reg_mov(need, n + (F0 + layer * NT + 1))
                act.wait_ge(s_zero, 1)
                act.wait_ge(transformed, need)
                if layer == 0:
                    act.wait_ge(hidden_out, 16 * n + 16 * F0)
                    act.activation(result[:, :], ps_out[:, :], ACT.Relu).then_inc(result_ready, 1)
                else:
                    act.activation(sums[0:NODES, 0, bass.ds(n * NC, D)], ps_out[:, :], ACT.Identity,
                                   accum_out=row_sum[:, bass.ds(n, 1)]).then_inc(stat, 1)
                    act.reg_mov(need, 2 * n + 1)
                    act.wait_ge(s_zero, 1)
                    act.wait_ge(stat, need)
                    act.activation(neg_mean[:, bass.ds(n, 1)], row_sum[:, bass.ds(n, 1)], ACT.Copy,
                                   scale=-1.0 / D).then_inc(stat, 1)
                    act.reg_mov(need, 2 * n + 2)
                    act.wait_ge(s_zero, 1)
                    act.wait_ge(stat, need)
                    act.activation(ps_out[:, :], ps_out[:, :], ACT.Square, bias=neg_mean[:, bass.ds(n, 1)],
                                   accum_out=square_sum[:, bass.ds(n, 1)]).then_inc(result_ready, 1)

            act.wait_ge(s_last_row, 1)
            with act.Fori(0, NT) as n:
                pack(0, n)
                finish(0, n)
            with act.Fori(0, NT - 1) as n:
                pack(1, n)
                finish(1, n)
            pack(1, NT - 1)
            act.wait_ge(s_var, 1)
            act.activation(spread[:, 0:NT - 1], spread[:, 0:NT - 1], ACT.Sqrt).then_inc(s_sd, 1)
            act.wait_ge(s_rstd, 2)
            for n in range(FIRST, NT - 1):
                y = sums[0:NODES, 0, n * NC:n * NC + D]
                act.activation(y, y, ACT.Identity, bias=row_sum[:, n:n + 1],
                               scale=spread[:, n:n + 1]).then_inc(s_norm_a, 1)
            finish(1, NT - 1)
            act.wait_ge(s_var, 2)
            act.activation(spread[:, NT - 1:NT], spread[:, NT - 1:NT], ACT.Sqrt).then_inc(s_sd, 1)

        @block.vector
        def _(dve):
            dve.memset(zero[:, :], 0.0).then_inc(s_zero, 1)
            dve.memset(ones[:, :], 1.0).then_inc(added, A0)
            dve.memset(src_col[:, TILES:LISTED], 0).then_inc(s_ends, 1)
            dve.memset(key_col[:, TILES:LISTED], 0).then_inc(s_ends, 1)
            dve.memset(sums[:, 1, 0:CLEAR_BLOCK], 0.0).then_inc(s_block, 1)

            dve.wait_ge(s_dst, 16)
            lists = dst_list.rearrange("p (t e) -> p t e", t=LT)
            dve.tensor_reduce(least, lists, AX.X, ALU.min).then_inc(s_stats, 1)
            dve.tensor_reduce(most, lists, AX.X, ALU.max).then_inc(s_stats, 1)
            dve.wait_ge(s_stats, 2)
            dve.tensor_tensor(width, most, least, ALU.subtract).then_inc(s_stats, 1)
            dve.tensor_scalar(offset_f, least, float(R), None, ALU.mult).then_inc(s_offset, 1)
            dve.wait_ge(s_stats, 3)
            dve.tensor_reduce(widest, width, AX.X, ALU.max).then_inc(s_widest, 1)
            dve.wait_ge(s_src, 16)
            dve.tensor_copy(src_f, src_list).then_inc(s_list_f, 1)
            dve.wait_ge(s_widest_t, 1)
            dve.tensor_reduce(scalars_row[0:1, WIDTH:WIDTH + 1], ps_widest, AX.X, ALU.max).then_inc(s_width, 1)

            def tabulate(k, table):
                cols = table[:, 0:TILES].rearrange("p (q i) -> p i q", i=LT)
                for i in range(LT):
                    g = LT * k + i
                    dve.wait_ge(s_turned, g + 1)
                    dve.tensor_copy(cols[:, i, :], banks[g % OH][:, 0:LP]).then_inc(s_tables, 1)

            def stage(table, now, buf, column):
                return dve.tensor_copy(now[:, buf, :], table[:, bass.ds(column, RING)])

            tabulate(0, src_col)
            dve.wait_ge(s_tables, LT)
            dve.wait_ge(s_ends, 2)
            stage(src_col, src_now, 0, 0).then_inc(staged, 1)
            for i in range(LT):
                e = slice(i * P, (i + 1) * P)
                op = dve.tensor_scalar(key_f[:, e], dst_list[:, e], least[:, i:i + 1], float(R), ALU.subtract, ALU.mult)
            op.then_inc(s_stats, 1)
            dve.wait_ge(s_typ, 16)
            dve.wait_ge(s_stats, 4)
            dve.tensor_tensor(key_f, key_f, typ_list, ALU.add).then_inc(s_list_f, 1)
            dve.wait_ge(s_iota, 1)
            dve.tensor_copy(ps_iota[:, :], onehot[:, 0, :]).then_inc(s_iota_ps, 1)
            tabulate(1, key_col)
            dve.memset(sums[:, 1, CLEAR_POOL:ACC], 0.0).then_inc(cleared_dve, 1)
            dve.wait_ge(s_off_ld, 32)
            dve.wait_ge(s_limits, 2)
            dve.scalar_tensor_tensor(out=tile_no, in0=offsets_nt, scalar=limit, in1=tile_no,
                                     op0=ALU.is_lt, op1=ALU.mult).then_inc(s_reach, 1)
            dve.wait_ge(s_reach, 1)
            dve.tensor_reduce(last_f, tile_no, AX.X, ALU.max).then_inc(s_last_f, 1)
            dve.wait_ge(s_last_t, 1)
            dve.tensor_copy(scalars_row[0:1, LAST:LAST + NT], ps_last).then_inc(s_last_row, 1)
            dve.wait_ge(s_tables, 2 * LT)
            dve.wait_ge(s_iota_ps, 1)
            dve.wait_ge(s_width, 1)
            passes = dve.value_load(scalars_row[0:1, WIDTH:WIDTH + 1], min_val=0, max_val=N) // SPAN

            def make_onehot(oh, key):
                return dve.tensor_scalar(onehot[:, oh, :], ps_iota[:, :], key, None, ALU.is_equal)

            def add(product_buf, offset):
                part = sums[:, :, bass.ds(offset, COLS)]
                return dve.tensor_tensor(part, part, product[product_buf][:, :, :], ALU.add)

            def wait_clear(layer):
                if layer == 0:
                    dve.wait_ge(cleared, 1)
                    dve.wait_ge(cleared_pool, 1)
                    dve.wait_ge(cleared_dma, 16 * 3)
                    dve.wait_ge(cleared_dve, 1)
                    dve.wait_ge(s_block, 1)
                else:
                    dve.wait_ge(cleared, 1 + NT)

            at = dve.alloc_register("at")
            offs = [dve.alloc_register(f"offset{j}") for j in range(LOAD)]
            for layer in range(2):
                T0 = layer * TILES
                if layer:
                    stage(src_col, src_now, 0, 0).then_inc(staged, 1)
                with dve.If(passes > 0):
                    wait_clear(layer)
                    dve.memset(shift[:, :], 0.0).then_inc(x_dve, 1)
                    dve.wait_ge(x_dve, 1)
                    dve.sem_clear(x_dve)
                    with dve.Fori(0, passes) as p:
                        dve.tensor_scalar(shift[:, :], shift[:, :], float(COLS), None, ALU.add).then_inc(x_dve, 1)
                        dve.wait_ge(x_dve, 1)
                        dve.sem_clear(x_dve)
                        with dve.Fori(0, TILES) as t:
                            dve.tensor_copy(src_now[:, 1, 0:1], src_col[:, bass.ds(t, 1)]).then_inc(x_staged, 1)
                            dve.tensor_copy(key_now[:, 1, 0:1], key_col[:, bass.ds(t, 1)]).then_inc(x_dve, 1)
                            dve.wait_ge(x_dve, 1)
                            dve.sem_clear(x_dve)
                            dve.tensor_scalar(onehot[:, 0, :], ps_iota[:, :], shift[:, 0:1], key_now[:, 1, 0:1],
                                              ALU.add, ALU.is_equal).then_inc(x_hot, 1)
                            base = dve.value_load(offset_row[0:1, bass.ds(t, 1)], min_val=0, max_val=N * R)
                            dve.reg_alu(at, dve.to_reg(base + (p + 1) * COLS), N * R, ALU.min)
                            dve.wait_ge(x_multiplied, 1)
                            dve.sem_clear(x_multiplied)
                            add(0, dve.snap(at, min_val=0, max_val=N * R)).then_inc(x_dve, 1)
                            dve.wait_ge(x_dve, 1)
                            dve.sem_clear(x_dve)
                stage(key_col, key_now, 0, 0).then_inc(keyed, 1)
                wait_clear(layer)
                with dve.Fori(0, LOOPS) as c:
                    for j in range(BODY + 2):
                        if j < BODY:
                            if j == 0:
                                stage(src_col, src_now, 1, c * BODY + RING).then_inc(staged, 1)
                                stage(key_col, key_now, 1, c * BODY + RING).then_inc(keyed, 1)
                            if j % RING == 0:
                                dve.wait_ge(keyed, BODY // RING * c + (layer * STAGINGS + j // RING + 1))
                            dve.wait_ge(multiplied, BODY * c + (M0 + T0 + j - OH + 1))
                            make_onehot(j % OH, key_now[:, j // RING % 2, j % RING:j % RING + 1]).then_inc(hot, 1)
                        if j >= 2:
                            i = j - 2
                            if i % LOAD == 0:
                                some = min(LOAD, BODY - i)
                                dve.reg_load(offs[:some], offset_row[0:1, bass.ds(c * BODY + i, some)])
                            dve.wait_ge(multiplied, BODY * c + (M0 + T0 + i + 1))
                            dve.wait_ge(added, BODY * c + (A0 + T0 + i))
                            add(i % OH, dve.snap(offs[i % LOAD], min_val=0, max_val=N * R)).then_inc(added, 1)
                            if i % RING == RING - 1 and i < BODY - 1:
                                buf = i // RING % 2
                                stage(src_col, src_now, buf, c * BODY + i + 1 + RING).then_inc(staged, 1)
                                stage(key_col, key_now, buf, c * BODY + i + 1 + RING).then_inc(keyed, 1)
                dve.wait_ge(keyed, (layer + 1) * STAGINGS)
                make_onehot((TILES - 1) % OH, key_now[:, 0, 0:1]).then_inc(hot, 1)
                last_offset = dve.value_load(offset_row[0:1, TILES - 1:TILES], min_val=0, max_val=N * R)
                dve.wait_ge(multiplied, M0 + T0 + TILES)
                dve.wait_ge(added, A0 + T0 + TILES - 1)
                add((TILES - 1) % OH, last_offset).then_inc(added, 1)

            for g, (a, z) in enumerate(((0, NT - 1), (NT - 1, NT))):
                dve.wait_ge(result_ready, F0 + NT + z)
                dve.tensor_scalar(spread[:, a:z], square_sum[:, a:z], 1.0 / D, EPS, ALU.mult, ALU.add).then_inc(s_var, 1)
                dve.wait_ge(s_sd, g + 1)
                dve.reciprocal(spread[:, a:z], spread[:, a:z]).then_inc(s_rstd, 1)
                dve.wait_ge(s_rstd, 1 + 2 * g)
                if g == 0:
                    dve.tensor_tensor(row_sum[:, a:z], neg_mean[:, a:z], spread[:, a:z], ALU.mult).then_inc(s_rstd, 1)
                for n in range(0, FIRST) if g == 0 else (NT - 1,):
                    y = sums[0:NODES, 0, n * NC:n * NC + D]
                    dve.tensor_scalar(y, y, neg_mean[:, n:n + 1], spread[:, n:n + 1], ALU.add,
                                      ALU.mult).then_inc(s_norm_v, 1)


_INS = ['x', 'src', 'dst', 'edge_type_8', 'L0_gnn_W1', 'L0_gnn_self_w1', 'L0_gnn_b1', 'L0_gnn_W2', 'L0_gnn_self_w2', 'L0_gnn_b2']


def kernel(**inputs):
    import numpy as _np
    import concourse.bacc as _bacc
    from concourse import mybir as _mybir
    from concourse.bass_utils import run_bass_kernel_spmd as _run

    nc = _bacc.Bacc("TRN2", target_bir_lowering=False, num_devices=1)
    arrays, args = {}, []
    for name in _INS:
        a = _np.ascontiguousarray(inputs[name])
        arrays[f"in_{name}_dram"] = a
        args.append(nc.dram_tensor(f"in_{name}_dram", a.shape, _mybir.dt.from_np(a.dtype), kind="ExternalInput").ap())
    args.append(nc.dram_tensor("out_dram", tuple(inputs['x'].shape), _mybir.dt.float32, kind="ExternalOutput").ap())
    gnn_resnorm(nc, *args)
    r = _run(nc, [arrays], core_ids=[0])
    return r.results[0]["out_dram"]
```

```python
from contextlib import ExitStack

import concourse.bass as bass
from concourse import mybir

F32 = mybir.dt.float32
I32 = mybir.dt.int32
U32 = mybir.dt.uint32
ALU = mybir.AluOpType
ACT = mybir.ActivationFunctionType
AX = mybir.AxisListType


def gnn_resnorm(nc, x, src, dst, edge_type, w1, self_w1, b1, w2, self_w2, b2, out):
    N, D = x.shape
    E = src.shape[0]
    R = w1.shape[0]
    P = 128
    HALVES = D // P
    TILES = E // P
    SPAN = 12
    COLS = SPAN * R
    NODES = 125
    NT = N // NODES
    NC = NODES * R
    LP = 125
    LT = TILES // LP
    RING = 13
    BODY = 4 * RING
    LOOPS = TILES // BODY
    REST = TILES - LOOPS * BODY
    STAGINGS = LOOPS * BODY // RING + 2
    LISTED = STAGINGS * RING
    LOAD = 16
    OH = 4
    AHEAD = 2
    HOTS = LOOPS * BODY + AHEAD
    PIECES = 6
    EPS = 1e-5
    ACC = (N + SPAN) * R
    assert HALVES == 2 and TILES * P == E and NT * NODES == N and LP * LT == TILES
    assert REST == 1 and COLS <= P and RING // 2 == PIECES

    with ExitStack() as ctx:
        def sb(name, shape, dt):
            return ctx.enter_context(nc.sbuf_tensor(name, shape, dt))

        def ps(name, shape, dt=F32):
            return ctx.enter_context(nc.psum_tensor(name, shape, dt))

        def sem(name):
            return ctx.enter_context(nc.semaphore(name))

        sums = sb("sums", [P, HALVES, ACC], F32)
        weights = sb("weights", [P, R + 1, HALVES, D], F32)
        rows = sb("rows", [P, RING, D], F32)
        onehot = sb("onehot", [P, OH, COLS], F32)
        packed = sb("packed", [P, HALVES, R, NODES], F32)
        own = sb("own", [NODES, D], F32)
        own_t = sb("own_t", [P, HALVES, NODES], F32)
        result = sb("result", [NODES + 1, D], F32)
        src_col = sb("src_col", [P, LISTED], mybir.dt.uint16)
        key_col = sb("key_col", [P, LISTED], mybir.dt.uint16)
        src_now = sb("src_now", [P, 2, RING], U32)
        key_now = sb("key_now", [P, 2, RING], F32)
        ident = sb("ident", [P, P], F32)
        single = sb("single", [33, TILES + 7], F32)
        offset_row = single[0:1, :].bitcast(I32)
        bias = single[32:33, 0:D]
        ones = single[32:33, D:D + P]
        zero = sb("zero", [P, 1], F32)
        scalars_row = sb("scalars_row", [1, 32], I32)
        shift = sb("shift", [P, 1], F32)
        row_sum = sb("row_sum", [NODES, NT], F32)
        neg_mean = sb("neg_mean", [NODES, NT], F32)
        square_sum = sb("square_sum", [NODES, NT], F32)
        spread = sb("spread", [NODES, NT], F32)
        eps = sb("eps", [NODES, 1], F32)
        minus_one = sb("minus_one", [NODES, 1], F32)

        prep = weights.rearrange("p a b c -> p (a b c)")
        L = LT * P
        dst_list, src_list, typ_list = (prep[0:LP, i * L:(i + 1) * L].bitcast(I32) for i in range(3))
        src_f, key_f = (prep[0:LP, i * L:(i + 1) * L] for i in range(3, 5))
        tile_no = prep[0:NT, 5 * L:5 * L + TILES]
        offsets_nt = prep[0:NT, 5 * L + TILES:5 * L + 2 * TILES].bitcast(I32)
        at = 5 * L + 2 * TILES
        least, most, width = (prep[0:LP, at + i * LT:at + (i + 1) * LT] for i in range(3))
        offset_f = prep[0:LP, at + 3 * LT:at + 4 * LT].bitcast(I32)
        widest = prep[0:LP, at + 4 * LT:at + 4 * LT + 1]
        limit = prep[0:NT, at + 4 * LT + 1:at + 4 * LT + 2]
        last_f = prep[0:NT, at + 4 * LT + 2:at + 4 * LT + 3]

        banks = [ps(f"bank{i}", [P, 512]) for i in range(OH + 4)]
        product = [banks[i][:, 0:HALVES * COLS].rearrange("p (h c) -> p h c", h=HALVES) for i in range(OH)]
        ps_out = banks[OH][0:NODES, 0:D]
        ps_own = banks[OH + 1][:, 0:HALVES * NODES].rearrange("p (h c) -> p h c", h=HALVES)
        ps_iota = banks[OH + 2][:, 0:COLS]
        ps_widest = banks[OH + 3][0:1, 0:LP]
        ps_last = banks[OH][0:1, 0:NT]

        hidden = nc.dram_tensor("hidden", (N, D), F32).ap()
        offset_dram = nc.dram_tensor("offset_dram", (1, TILES), I32).ap()

        s_dst = sem("s_dst")
        s_src = sem("s_src")
        s_typ = sem("s_typ")
        s_const = sem("s_const")
        s_zero = sem("s_zero")
        s_eps = sem("s_eps")
        s_iota = sem("s_iota")
        s_iota_ps = sem("s_iota_ps")
        s_ends = sem("s_ends")
        s_block = sem("s_block")
        s_stats = sem("s_stats")
        s_offset = sem("s_offset")
        s_off_st = sem("s_off_st")
        s_off_ld = sem("s_off_ld")
        s_widest = sem("s_widest")
        s_widest_t = sem("s_widest_t")
        s_width = sem("s_width")
        s_src_f = sem("s_src_f")
        s_key_f = sem("s_key_f")
        s_turned = sem("s_turned")
        s_tables = sem("s_tables")
        s_limits = sem("s_limits")
        s_reach = sem("s_reach")
        s_last_f = sem("s_last_f")
        s_last_t = sem("s_last_t")
        s_last_row = sem("s_last_row")
        staged = sem("staged")
        keyed = sem("keyed")
        landed = [sem(f"landed{j}") for j in range(RING)]
        hot = sem("hot")
        multiplied = sem("multiplied")
        added = sem("added")
        weights_in = sem("weights_in")
        own_in = sem("own_in")
        residual_in = sem("residual_in")
        own_turned = sem("own_turned")
        own_t_ready = sem("own_t_ready")
        packed_ready = sem("packed_ready")
        cleared = sem("cleared")
        cleared_pool = sem("cleared_pool")
        cleared_dve = sem("cleared_dve")
        cleared_dma = sem("cleared_dma")
        transformed = sem("transformed")
        result_ready = sem("result_ready")
        hidden_out = sem("hidden_out")
        stat = sem("stat")
        x_staged = sem("x_staged")
        x_landed = sem("x_landed")
        x_hot = sem("x_hot")
        x_multiplied = sem("x_multiplied")
        x_dve = sem("x_dve")
        x_over = sem("x_over")
        s_sd = sem("s_sd")
        s_rstd_p = sem("s_rstd_p")
        s_rstd_v = sem("s_rstd_v")
        s_norm_p = sem("s_norm_p")
        s_norm_a = sem("s_norm_a")
        s_norm_v = sem("s_norm_v")
        s_out = sem("s_out")

        block = ctx.enter_context(nc.Block())

        LAST, WIDTH = 0, NT
        BY_POOL = 9
        EARLY = NT - 2
        CLEAR_BLOCK = 1700
        COPIES = 6
        CLEAR_DMA = (COPIES + 1) * CLEAR_BLOCK
        CLEAR_POOL = 16600
        CLEAR_ACT = 2500
        M0, A0 = RING, OH
        F0 = 1

        def rows_before(layer, j):
            return layer * (LOOPS * BODY // RING + (1 if j < REST else 0)) * 16

        @block.sync
        def _(sp):
            sp.nop().then_inc(hidden_out, 16 * F0)
            sp.dma_start(dst_list, dst.rearrange("(p e) -> p e", p=LP)).then_inc(s_dst, 16)
            sp.dma_start(src_list, src.rearrange("(p e) -> p e", p=LP)).then_inc(s_src, 16)
            sp.dma_start(typ_list, edge_type.rearrange("(p e) -> p e", p=LP)).then_inc(s_typ, 16)
            sp.wait_ge(s_block, 1)

            def copy_block(i):
                at = i * CLEAR_BLOCK
                sp.dma_start(sums[:, 1, at:at + CLEAR_BLOCK], sums[:, 1, 0:CLEAR_BLOCK]).then_inc(cleared_dma, 16)

            copy_block(1)
            sp.wait_ge(s_offset, 1)
            sp.dma_start(offset_dram.rearrange("a (p t) -> (a p) t", p=LP), offset_f).then_inc(s_off_st, 16)
            copy_block(2)
            sp.wait_ge(s_off_st, 16)
            sp.dma_start(offset_row[:, 0:TILES], offset_dram).then_inc(s_off_ld, 16)
            sp.dma_start(offsets_nt, offset_dram.broadcast_to((NT, TILES))).then_inc(s_off_ld, 16)
            for i in range(3, COPIES + 1):
                copy_block(i)
            for layer, (w, sw, b, table) in enumerate(((w1, self_w1, b1, x), (w2, self_w2, b2, hidden))):
                if layer == 0:
                    sp.wait_ge(s_tables, 2 * LT)
                    sp.wait_ge(s_last_row, 1)
                else:
                    sp.wait_ge(transformed, F0 + layer * NT)
                for r in range(R):
                    sp.dma_start(weights[:, r, :, :], w[r].rearrange("(h p) o -> p h o", p=P)).then_inc(weights_in, 16)
                sp.dma_start(weights[:, R, :, :], sw.rearrange("(h p) o -> p h o", p=P)).then_inc(weights_in, 16)
                row = bias[:, :] if layer == 0 else result[NODES:NODES + 1, :]
                sp.dma_start(row, b.rearrange("(a o) -> a o", a=1)).then_inc(weights_in, 16)
                if layer:
                    sp.wait_ge(hidden_out, 16 * (F0 + NT))

                def load(n):
                    sp.wait_ge(own_turned, n + (F0 + layer * NT))
                    sp.dma_start(own[:, :], table[bass.ds(n * NODES, NODES), :]).then_inc(own_in, 16)
                    if layer == 1:
                        sp.wait_ge(transformed, n + (F0 + NT))
                        sp.dma_start(result[0:NODES, :], x[bass.ds(n * NODES, NODES), :]).then_inc(residual_in, 16)

                def store(n):
                    if layer == 0:
                        sp.wait_ge(result_ready, n + (F0 + 1))
                        sp.dma_start(hidden[bass.ds(n * NODES, NODES), :], result[0:NODES, :]).then_inc(hidden_out, 16)

                load(0)
                with sp.Fori(0, NT - 1) as n:
                    load(n + 1)
                    store(n)
                store(NT - 1)
            normal = sums[:, 0, 0:N * R].rearrange("p (n c) -> p n c", n=NT)[:, :, 0:D]
            out_v = out.rearrange("(n p) d -> p n d", p=NODES)
            cut = NODES // 16 * 16
            for done, count, a, z in ((s_norm_p, BY_POOL, 0, BY_POOL), (s_norm_a, EARLY - BY_POOL, BY_POOL, EARLY),
                                      (s_norm_v, 1, EARLY, EARLY + 1), (s_norm_v, 2, EARLY + 1, NT)):
                sp.wait_ge(done, count)
                sp.dma_start(out_v[0:cut, a:z, :], normal[0:cut, a:z, :]).then_inc(s_out, 16)
                sp.dma_start(out_v[cut:NODES, a:z, :], normal[cut:NODES, a:z, :]).then_inc(s_out, 16)
            sp.wait_ge(s_out, 8 * 16)

        @block.gpsimd
        def _(pool):
            pool.memset(ident[:, :], 0.0).then_inc(s_const, 1)
            pool.wait_ge(s_const, 1)
            pool.affine_select(out=ident[:, :], in_=ident[:, :], compare_op=ALU.not_equal, fill=1.0,
                               base=0, pattern=[[-1, P]], channel_multiplier=1).then_inc(s_const, 1)
            pool.wait_ge(s_const, 2)
            pool.affine_select(out=ident[:, :], in_=ident[:, :], compare_op=ALU.not_equal, fill=1.0,
                               base=-NODES, pattern=[[0, P]], channel_multiplier=1).then_inc(s_const, 1)
            pool.iota(onehot[:, 0, :], [[1, COLS]], base=0, channel_multiplier=0,
                      allow_small_or_imprecise_dtypes=True).then_inc(s_iota, 1)
            pool.iota(tile_no, [[1, TILES]], base=1, channel_multiplier=0,
                      allow_small_or_imprecise_dtypes=True).then_inc(s_limits, 1)
            pool.iota(limit, [[1, 1]], base=NC, channel_multiplier=NC,
                      allow_small_or_imprecise_dtypes=True).then_inc(s_limits, 1)
            pool.memset(sums[:, 1, CLEAR_DMA:CLEAR_POOL], 0.0).then_inc(cleared_pool, 1)

            def gather(table, buf, index):
                return pool.indirect_dma_start(out=rows[:, buf, :], out_offset=None, in_=table,
                                               in_offset=bass.IndirectOffsetOnAxis(ap=index, axis=0))

            pool.wait_ge(s_width, 1)
            passes = pool.value_load(scalars_row[0:1, WIDTH:WIDTH + 1], min_val=0, max_val=N) // SPAN
            need = pool.alloc_register("need")
            for layer, table in enumerate((x, hidden)):
                if layer:
                    pool.wait_ge(hidden_out, 16 * (F0 + NT))
                with pool.If(passes > 0):
                    with pool.Fori(0, passes):
                        with pool.Fori(0, TILES):
                            pool.wait_ge(x_staged, 1)
                            pool.sem_clear(x_staged)
                            gather(table, 0, src_now[:, 1, 0:1]).then_inc(x_landed, 16)
                    pool.wait_ge(x_over, layer + 1)
                with pool.Fori(0, LOOPS) as c:
                    for j in range(BODY):
                        if j % RING == 0:
                            pool.wait_ge(staged, BODY // RING * c + (layer * STAGINGS + j // RING + 1))
                        pool.reg_mov(need, BODY * c + (M0 + layer * TILES + j - RING + 1))
                        pool.wait_ge(s_width, 1)
                        pool.wait_ge(multiplied, need)
                        gather(table, j % RING, src_now[:, j // RING % 2, j % RING:j % RING + 1]).then_inc(landed[j % RING], 16)
                pool.wait_ge(staged, layer * STAGINGS + LOOPS * BODY // RING + 1)
                pool.wait_ge(multiplied, M0 + layer * TILES + TILES - RING)
                gather(table, 0, src_now[:, 0, 0:1]).then_inc(landed[0], 16)

            pool.wait_ge(s_eps, 2)
            pool.wait_ge(s_sd, 1)
            pool.tensor_tensor(spread[:, 0:EARLY], spread[:, 0:EARLY],
                               minus_one[:, 0:1].broadcast_to((NODES, EARLY)), ALU.pow).then_inc(s_rstd_p, 1)
            pool.wait_ge(s_rstd_p, 1)
            pool.tensor_tensor(row_sum[:, 0:EARLY], neg_mean[:, 0:EARLY], spread[:, 0:EARLY],
                               ALU.mult).then_inc(s_rstd_p, 1)
            for n in range(BY_POOL):
                y = sums[0:NODES, 0, n * NC:n * NC + D]
                pool.tensor_scalar(y, y, neg_mean[:, n:n + 1], spread[:, n:n + 1], ALU.add,
                                   ALU.mult).then_inc(s_norm_p, 1)

        @block.tensor
        def _(pe):
            pe.nop().then_inc(multiplied, M0)
            pe.nop().then_inc(transformed, F0)
            pe.nop().then_inc(own_turned, F0)
            pe.wait_ge(s_const, 3)
            for k, (lst, ready) in enumerate(((src_f, s_src_f), (key_f, s_key_f))):
                pe.wait_ge(ready, 1)
                for i in range(LT):
                    g = LT * k + i
                    if g >= OH:
                        pe.wait_ge(s_tables, g - OH + 1)
                    pe.transpose(banks[g % OH][:, 0:LP], lst[:, i * P:(i + 1) * P],
                                 ident[0:LP, 0:LP]).then_inc(s_turned, 1)
                    if g == 1:
                        pe.wait_ge(s_widest, 1)
                        pe.transpose(ps_widest, widest, ident[0:LP, 0:LP]).then_inc(s_widest_t, 1)
            pe.wait_ge(s_last_f, 1)
            pe.transpose(ps_last, last_f, ident[0:NT, 0:NT]).then_inc(s_last_t, 1)

            pe.wait_ge(s_width, 1)
            passes = pe.value_load(scalars_row[0:1, WIDTH:WIDTH + 1], min_val=0, max_val=N) // SPAN
            pe.wait_ge(s_last_row, 1)
            CUTS = [0, 0, 4, 8, 12, 15, 16]
            node = pe.alloc_register("node")
            last = pe.alloc_register("last")
            gathered = pe.alloc_register("gathered")
            pe.reg_mov(gathered, 0)

            def turn_own(layer, n):
                pe.wait_ge(own_in, 16 * n + 16 * (layer * NT + 1))
                for h in range(HALVES):
                    mm = pe.transpose(ps_own[:, h, :], own[:, h * P:(h + 1) * P], ident[0:NODES, 0:NODES])
                mm.then_inc(own_turned, 1)

            def add_own(layer, n, start):
                pe.wait_ge(own_t_ready, n + (layer * NT + 1))
                for h in range(HALVES):
                    pe.matmul(ps_out[:, :], own_t[:, h, :], weights[:, R, h, :], start=start and h == 0, stop=False)

            def add_bias(layer, n, stop):
                if layer == 0:
                    return pe.matmul(ps_out[:, :], ones[:, 0:NODES], bias[:, :], start=False, stop=stop)
                pe.wait_ge(residual_in, 16 * n + 16)
                return pe.matmul(ps_out[:, :], ident[0:NODES + 1, 0:NODES], result[:, :], start=False, stop=stop)

            def await_out(layer, n):
                pe.wait_ge(weights_in, 16 * (R + 2) * (layer + 1))
                pe.wait_ge(result_ready, n + (F0 + layer * NT))

            parts = [(h, r) for h in range(HALVES) for r in range(R)]

            def piece(layer, k):
                n = pe.snap(node, min_val=0, max_val=NT - 1)
                if k == 0:
                    turn_own(layer, n)
                if CUTS[k] == 0 and CUTS[k + 1] > 0:
                    await_out(layer, n)
                for h, r in parts[CUTS[k]:CUTS[k + 1]]:
                    if r == 0:
                        pe.wait_ge(packed_ready, 2 * n + (2 * layer * (NT - 1) + h + 1))
                    pe.matmul(ps_out[:, :], packed[:, h, r, :], weights[:, r, h, :], start=(h, r) == parts[0], stop=False)
                if k == PIECES - 1:
                    add_own(layer, n, False)
                    add_bias(layer, n, True).then_inc(transformed, 1)

            def multiply(buf, oh, hot_need, landed_need, added_need):
                pe.wait_ge(hot, hot_need)
                pe.wait_ge(landed[buf], landed_need)
                pe.wait_ge(added, added_need)
                for h in range(HALVES):
                    mm = pe.matmul(product[oh][:, h, :], rows[:, buf, h * P:(h + 1) * P], onehot[:, oh, :],
                                   start=True, stop=True)
                mm.then_inc(multiplied, 1)

            for layer in range(2):
                with pe.If(passes > 0):
                    with pe.Fori(0, passes):
                        with pe.Fori(0, TILES):
                            pe.wait_ge(x_hot, 1)
                            pe.sem_clear(x_hot)
                            pe.reg_add(gathered, gathered, 16)
                            pe.wait_ge(x_landed, pe.snap(gathered, min_val=16))
                            for h in range(HALVES):
                                mm = pe.matmul(product[0][:, h, :], rows[:, 0, h * P:(h + 1) * P],
                                               onehot[:, 0, :], start=True, stop=True)
                            mm.then_inc(x_multiplied, 1)
                pe.reg_mov(node, 0)
                pe.reg_load(last, scalars_row[0:1, LAST:LAST + 1])
                with pe.Fori(0, LOOPS) as c:
                    for j in range(BODY):
                        t0 = layer * TILES + j
                        multiply(j % RING, j % OH,
                                 BODY * c + (layer * HOTS + j + 1),
                                 16 * BODY // RING * c + (rows_before(layer, j % RING) + 16 * (j // RING + 1)),
                                 BODY * c + (A0 + t0 + 1 - OH))
                        if j % RING % 2 == 0 and j % RING < 2 * PIECES:
                            q, k = j // RING, (j % RING) // 2
                            done = BODY * c + RING * q
                            with pe.If(pe.snap(last, min_val=0, max_val=TILES) <= done):
                                piece(layer, k)
                                if k == PIECES - 1:
                                    pe.reg_add(node, node, 1)
                                    pe.reg_load(last, scalars_row[0:1, bass.ds(pe.snap(node, min_val=0, max_val=NT - 1), 1)])
                with pe.If(pe.snap(node, min_val=0, max_val=NT - 1) >= NT - 1):
                    turn_own(layer, NT - 1)
                multiply(0, (LOOPS * BODY) % OH, layer * HOTS + TILES,
                         rows_before(layer + 1, 0), A0 + (layer + 1) * TILES - OH)
                first = pe.snap(node, min_val=0, max_val=NT - 1)
                with pe.If(first < NT - 1):
                    with pe.Fori(first, NT - 1) as m:
                        pe.reg_mov(node, m)
                        for k in range(PIECES):
                            piece(layer, k)
                    turn_own(layer, NT - 1)
                await_out(layer, NT - 1)
                add_own(layer, NT - 1, True)
                if layer == 0:
                    add_bias(layer, NT - 1, False)
                pe.wait_ge(added, A0 + (layer + 1) * TILES)
                for h, r in parts:
                    final = sums[:, h, (NT - 1) * NC:NT * NC].rearrange("p (m r) -> p r m", r=R)
                    mm = pe.matmul(ps_out[:, :], final[:, r, :], weights[:, r, h, :], start=False,
                                   stop=layer == 0 and (h, r) == parts[-1])
                if layer:
                    mm = add_bias(layer, NT - 1, True)
                mm.then_inc(transformed, 1)

        @block.scalar
        def _(act):
            act.nop().then_inc(result_ready, F0)
            act.wait_ge(s_zero, 1)
            act.activation(sums[:, 0, 0:CLEAR_ACT], zero[:, 0:1].broadcast_to((P, CLEAR_ACT)), ACT.Copy).then_inc(cleared, 1)
            act.wait_ge(s_src, 16)
            act.activation(src_f, src_list, ACT.Copy).then_inc(s_src_f, 1)
            act.activation(sums[:, 0, CLEAR_ACT:ACC], zero[:, 0:1].broadcast_to((P, ACC - CLEAR_ACT)), ACT.Copy).then_inc(cleared, 1)
            need = act.alloc_register("need")

            def pack(layer, n):
                final = act.value_load(scalars_row[0:1, bass.ds(n, 1)], min_val=0, max_val=TILES)
                act.reg_mov(need, final + (A0 + layer * TILES))
                act.wait_ge(s_zero, 1)
                act.wait_ge(added, need)
                for h in range(HALVES):
                    act.activation(packed[:, h, :, :],
                                   sums[:, h, bass.ds(n * NC, NC)].rearrange("p (m r) -> p r m", r=R),
                                   ACT.Copy).then_inc(packed_ready, 1)

            def copy_own(layer, n):
                act.wait_ge(own_turned, n + (F0 + layer * NT + 1))
                act.activation(own_t[:, :, :], ps_own[:, :, :], ACT.Copy).then_inc(own_t_ready, 1)

            def clear(n):
                act.activation(sums[:, :, bass.ds(n * NC, NC)],
                               zero[:, None, 0:1].broadcast_to((P, HALVES, NC)), ACT.Copy).then_inc(cleared, 1)

            def await_transformed(layer, n):
                act.reg_mov(need, n + (F0 + layer * NT + 1))
                act.wait_ge(s_zero, 1)
                act.wait_ge(transformed, need)

            def relu(n):
                await_transformed(0, n)
                act.wait_ge(hidden_out, 16 * n + 16 * F0)
                act.activation(result[0:NODES, :], ps_out[:, :], ACT.Relu).then_inc(result_ready, 1)

            def take(n):
                await_transformed(1, n)
                act.activation(sums[0:NODES, 0, bass.ds(n * NC, D)], ps_out[:, :], ACT.Identity,
                               accum_out=row_sum[:, bass.ds(n, 1)]).then_inc(result_ready, 1)

            def measure(n):
                act.reg_mov(need, n + (F0 + NT + 1))
                act.wait_ge(s_zero, 1)
                act.wait_ge(result_ready, need)
                act.activation(neg_mean[:, bass.ds(n, 1)], row_sum[:, bass.ds(n, 1)], ACT.Copy,
                               scale=-1.0 / D).then_inc(stat, 1)
                act.reg_mov(need, 2 * n + 1)
                act.wait_ge(s_zero, 1)
                act.wait_ge(stat, need)
                act.activation(sums[0:NODES, 1, bass.ds(n * NC, D)], sums[0:NODES, 0, bass.ds(n * NC, D)],
                               ACT.Square, bias=neg_mean[:, bass.ds(n, 1)],
                               accum_out=square_sum[:, bass.ds(n, 1)]).then_inc(stat, 1)

            def deviation(a, z):
                act.wait_ge(stat, 2 * z)
                act.activation(spread[:, a:z], square_sum[:, a:z], ACT.Sqrt, bias=eps[:, 0:1],
                               scale=1.0 / D).then_inc(s_sd, 1)

            act.wait_ge(s_last_row, 1)
            with act.Fori(0, NT - 1) as n:
                pack(0, n)
                copy_own(0, n)
                act.reg_mov(need, 2 * n + 2)
                act.wait_ge(s_zero, 1)
                act.wait_ge(packed_ready, need)
                clear(n)
                relu(n)
            copy_own(0, NT - 1)
            relu(NT - 1)
            clear(NT - 1)
            pack(1, 0)
            copy_own(1, 0)
            with act.Fori(0, EARLY) as n:
                take(n)
                pack(1, n + 1)
                copy_own(1, n + 1)
                measure(n)
            act.wait_ge(s_eps, 1)
            deviation(0, EARLY)
            take(EARLY)
            copy_own(1, NT - 1)
            measure(EARLY)
            deviation(EARLY, NT - 1)
            act.wait_ge(s_rstd_p, 2)
            for n in range(BY_POOL, EARLY):
                y = sums[0:NODES, 0, n * NC:n * NC + D]
                act.activation(y, y, ACT.Identity, bias=row_sum[:, n:n + 1],
                               scale=spread[:, n:n + 1]).then_inc(s_norm_a, 1)
            take(NT - 1)
            measure(NT - 1)
            deviation(NT - 1, NT)

        @block.vector
        def _(dve):
            dve.memset(zero[:, :], 0.0).then_inc(s_zero, 1)
            dve.memset(ones[:, :], 1.0).then_inc(added, A0)
            dve.memset(src_col[:, TILES:LISTED], 0).then_inc(s_ends, 1)
            dve.memset(key_col[:, TILES:LISTED], 0).then_inc(s_ends, 1)
            dve.memset(eps[:, :], EPS).then_inc(s_eps, 1)
            dve.memset(minus_one[:, :], -1.0).then_inc(s_eps, 1)
            dve.memset(sums[:, 1, 0:CLEAR_BLOCK], 0.0).then_inc(s_block, 1)
            dve.wait_ge(s_dst, 16)
            lists = dst_list.rearrange("p (t e) -> p t e", t=LT)
            dve.tensor_reduce(least, lists, AX.X, ALU.min).then_inc(s_stats, 1)
            dve.tensor_reduce(most, lists, AX.X, ALU.max).then_inc(s_stats, 1)
            dve.wait_ge(s_stats, 2)
            dve.tensor_tensor(width, most, least, ALU.subtract).then_inc(s_stats, 1)
            dve.tensor_scalar(offset_f, least, float(R), None, ALU.mult).then_inc(s_offset, 1)
            dve.wait_ge(s_stats, 3)
            dve.tensor_reduce(widest, width, AX.X, ALU.max).then_inc(s_widest, 1)

            def tabulate(k, table):
                cols = table[:, 0:TILES].rearrange("p (q i) -> p i q", i=LT)
                for i in range(LT):
                    g = LT * k + i
                    dve.wait_ge(s_turned, g + 1)
                    dve.tensor_copy(cols[:, i, :], banks[g % OH][:, 0:LP]).then_inc(s_tables, 1)
                    if g == 1:
                        dve.wait_ge(s_widest_t, 1)
                        dve.tensor_reduce(scalars_row[0:1, WIDTH:WIDTH + 1], ps_widest, AX.X, ALU.max).then_inc(s_width, 1)

            def stage(table, now, buf, column):
                return dve.tensor_copy(now[:, buf, :], table[:, bass.ds(column, RING)])

            tabulate(0, src_col)
            dve.wait_ge(s_tables, LT)
            dve.wait_ge(s_ends, 2)
            stage(src_col, src_now, 0, 0).then_inc(staged, 1)
            for i in range(LT):
                e = slice(i * P, (i + 1) * P)
                op = dve.tensor_scalar(key_f[:, e], dst_list[:, e], least[:, i:i + 1], float(R), ALU.subtract, ALU.mult)
            op.then_inc(s_stats, 1)
            dve.wait_ge(s_typ, 16)
            dve.wait_ge(s_stats, 4)
            dve.tensor_tensor(key_f, key_f, typ_list, ALU.add).then_inc(s_key_f, 1)
            dve.wait_ge(s_iota, 1)
            dve.tensor_copy(ps_iota[:, :], onehot[:, 0, :]).then_inc(s_iota_ps, 1)
            tabulate(1, key_col)
            dve.memset(sums[:, 1, CLEAR_POOL:ACC], 0.0).then_inc(cleared_dve, 1)
            dve.wait_ge(s_off_ld, 32)
            dve.wait_ge(s_limits, 2)
            dve.scalar_tensor_tensor(out=tile_no, in0=offsets_nt, scalar=limit, in1=tile_no,
                                     op0=ALU.is_lt, op1=ALU.mult).then_inc(s_reach, 1)
            dve.wait_ge(s_reach, 1)
            dve.tensor_reduce(last_f, tile_no, AX.X, ALU.max).then_inc(s_last_f, 1)
            dve.wait_ge(s_last_t, 1)
            dve.tensor_copy(scalars_row[0:1, LAST:LAST + NT], ps_last).then_inc(s_last_row, 1)
            dve.wait_ge(s_tables, 2 * LT)
            dve.wait_ge(s_iota_ps, 1)
            dve.wait_ge(s_width, 1)
            passes = dve.value_load(scalars_row[0:1, WIDTH:WIDTH + 1], min_val=0, max_val=N) // SPAN

            def make_onehot(oh, key):
                return dve.tensor_scalar(onehot[:, oh, :], ps_iota[:, :], key, None, ALU.is_equal)

            def add(product_buf, offset):
                part = sums[:, :, bass.ds(offset, COLS)]
                return dve.tensor_tensor(part, part, product[product_buf][:, :, :], ALU.add)

            def wait_clear(layer):
                if layer == 0:
                    dve.wait_ge(cleared, 2)
                    dve.wait_ge(cleared_pool, 1)
                    dve.wait_ge(cleared_dma, 16 * COPIES)
                    dve.wait_ge(cleared_dve, 1)
                    dve.wait_ge(s_block, 1)
                else:
                    dve.wait_ge(cleared, 2 + NT)

            at = dve.alloc_register("at")
            offs = [dve.alloc_register(f"offset{j}") for j in range(LOAD)]
            for layer in range(2):
                T0 = layer * TILES
                if layer:
                    dve.wait_ge(staged, layer * STAGINGS)
                    dve.wait_ge(keyed, layer * STAGINGS)
                    stage(src_col, src_now, 0, 0).then_inc(staged, 1)
                with dve.If(passes > 0):
                    wait_clear(layer)
                    dve.memset(shift[:, :], 0.0).then_inc(x_dve, 1)
                    dve.wait_ge(x_dve, 1)
                    dve.sem_clear(x_dve)
                    with dve.Fori(0, passes) as p:
                        dve.tensor_scalar(shift[:, :], shift[:, :], float(COLS), None, ALU.add).then_inc(x_dve, 1)
                        dve.wait_ge(x_dve, 1)
                        dve.sem_clear(x_dve)
                        with dve.Fori(0, TILES) as t:
                            dve.tensor_copy(src_now[:, 1, 0:1], src_col[:, bass.ds(t, 1)]).then_inc(x_staged, 1)
                            dve.tensor_copy(key_now[:, 1, 0:1], key_col[:, bass.ds(t, 1)]).then_inc(x_dve, 1)
                            dve.wait_ge(x_dve, 1)
                            dve.sem_clear(x_dve)
                            dve.tensor_scalar(onehot[:, 0, :], ps_iota[:, :], shift[:, 0:1], key_now[:, 1, 0:1],
                                              ALU.add, ALU.is_equal).then_inc(x_hot, 1)
                            base = dve.value_load(offset_row[0:1, bass.ds(t, 1)], min_val=0, max_val=N * R)
                            dve.reg_alu(at, dve.to_reg(base + (p + 1) * COLS), N * R, ALU.min)
                            dve.wait_ge(x_multiplied, 1)
                            dve.sem_clear(x_multiplied)
                            add(0, dve.snap(at, min_val=0, max_val=N * R)).then_inc(x_dve, 1)
                            dve.wait_ge(x_dve, 1)
                            dve.sem_clear(x_dve)
                    dve.nop().then_inc(x_over, 1)
                stage(key_col, key_now, 0, 0).then_inc(keyed, 1)
                stage(src_col, src_now, 1, RING).then_inc(staged, 1)
                stage(key_col, key_now, 1, RING).then_inc(keyed, 1)
                dve.wait_ge(keyed, layer * STAGINGS + 1)
                for t in range(AHEAD):
                    dve.wait_ge(multiplied, M0 + T0 - OH + t + 1)
                    make_onehot(t, key_now[:, 0, t:t + 1]).then_inc(hot, 1)
                wait_clear(layer)
                with dve.Fori(0, LOOPS) as c:
                    for j in range(BODY):
                        i = j + AHEAD
                        g = i // RING
                        if i % RING == 0:
                            dve.wait_ge(keyed, BODY // RING * c + (layer * STAGINGS + g + 1))
                        dve.wait_ge(multiplied, BODY * c + (M0 + T0 + i - OH + 1))
                        make_onehot(i % OH, key_now[:, g % 2, i % RING:i % RING + 1]).then_inc(hot, 1)
                        if j % LOAD == 0:
                            some = min(LOAD, BODY - j)
                            dve.reg_load(offs[:some], offset_row[0:1, bass.ds(c * BODY + j, some)])
                        dve.wait_ge(multiplied, BODY * c + (M0 + T0 + j + 1))
                        dve.wait_ge(added, BODY * c + (A0 + T0 + j))
                        add(j % OH, dve.snap(offs[j % LOAD], min_val=0, max_val=N * R)).then_inc(added, 1)
                        if j % RING == RING - 1:
                            buf = j // RING % 2
                            stage(src_col, src_now, buf, c * BODY + j + 1 + RING).then_inc(staged, 1)
                            stage(key_col, key_now, buf, c * BODY + j + 1 + RING).then_inc(keyed, 1)
                last_offset = dve.value_load(offset_row[0:1, TILES - 1:TILES], min_val=0, max_val=N * R)
                dve.wait_ge(multiplied, M0 + T0 + TILES)
                dve.wait_ge(added, A0 + T0 + TILES - 1)
                add((TILES - 1) % OH, last_offset).then_inc(added, 1)

            for g, n in enumerate(range(EARLY, NT)):
                dve.wait_ge(s_sd, g + 2)
                dve.reciprocal(spread[:, n:n + 1], spread[:, n:n + 1]).then_inc(s_rstd_v, 1)
                dve.wait_ge(s_rstd_v, g + 1)
                y = sums[0:NODES, 0, n * NC:n * NC + D]
                dve.tensor_scalar(y, y, neg_mean[:, n:n + 1], spread[:, n:n + 1], ALU.add,
                                  ALU.mult).then_inc(s_norm_v, 1)


_INS = ['x', 'src', 'dst', 'edge_type_8', 'L0_gnn_W1', 'L0_gnn_self_w1', 'L0_gnn_b1', 'L0_gnn_W2', 'L0_gnn_self_w2', 'L0_gnn_b2']


def kernel(**inputs):
    import numpy as _np
    import concourse.bacc as _bacc
    from concourse import mybir as _mybir
    from concourse.bass_utils import run_bass_kernel_spmd as _run

    nc = _bacc.Bacc("TRN2", target_bir_lowering=False, num_devices=1)
    arrays, args = {}, []
    for name in _INS:
        a = _np.ascontiguousarray(inputs[name])
        arrays[f"in_{name}_dram"] = a
        args.append(nc.dram_tensor(f"in_{name}_dram", a.shape, _mybir.dt.from_np(a.dtype), kind="ExternalInput").ap())
    args.append(nc.dram_tensor("out_dram", tuple(inputs['x'].shape), _mybir.dt.float32, kind="ExternalOutput").ap())
    gnn_resnorm(nc, *args)
    r = _run(nc, [arrays], core_ids=[0])
    return r.results[0]["out_dram"]
```
